# Optimizing a Trainium2 kernel written in Bass

```python
import numpy as np
import jax
import jax.numpy as jnp

def _softmax(x, axis=-1):
    return jax.nn.softmax(x, axis=axis)

def _gelu(x):
    return jax.nn.gelu(x, approximate=True)

def _silu(x):
    return jax.nn.silu(x)

def _sigmoid(x):
    return jax.nn.sigmoid(x)

def _layernorm(x, axis=-1, eps=1e-05):
    m = jnp.mean(x, axis=axis, keepdims=True)
    v = jnp.var(x, axis=axis, keepdims=True)
    return (x - m) / jnp.sqrt(v + eps)

def _scatter_add(tgt, idx, src, axis=0):
    return tgt.at[idx].add(src)

def _segment_sum(src, seg, n):
    return jax.ops.segment_sum(src, seg, n)
kernel_name = 'mk_rec_standalone_d1_rec_r8_a0e561'

def setup_inputs(seed: int=0):
    np.random.seed(seed)
    _w = jnp.asarray

    def _rec_inputs():
        import jax
        import jax.numpy as jnp
        _rk = jax.random.key(seed)
        r_X_dense = -0.000171701 + 0.999137 * jax.random.normal(jax.random.fold_in(_rk, 1), (1024, 13), jnp.float32)
        r_X_sparse = jnp.stack([jax.random.randint(jax.random.fold_in(jax.random.fold_in(_rk, 2), 0), (1024,), 1, 1000, jnp.int32), jax.random.randint(jax.random.fold_in(jax.random.fold_in(_rk, 2), 1), (1024,), 0, 7999, jnp.int32), jax.random.randint(jax.random.fold_in(jax.random.fold_in(_rk, 2), 2), (1024,), 7, 7999, jnp.int32), jax.random.randint(jax.random.fold_in(jax.random.fold_in(_rk, 2), 3), (1024,), 2, 7999, jnp.int32), jax.random.randint(jax.random.fold_in(jax.random.fold_in(_rk, 2), 4), (1024,), 1, 1000, jnp.int32), jax.random.randint(jax.random.fold_in(jax.random.fold_in(_rk, 2), 5), (1024,), 4, 1000, jnp.int32), jax.random.randint(jax.random.fold_in(jax.random.fold_in(_rk, 2), 6), (1024,), 2, 7991, jnp.int32), jax.random.randint(jax.random.fold_in(jax.random.fold_in(_rk, 2), 7), (1024,), 1, 7998, jnp.int32), jax.random.randint(jax.random.fold_in(jax.random.fold_in(_rk, 2), 8), (1024,), 4, 7999, jnp.int32), jax.random.randint(jax.random.fold_in(jax.random.fold_in(_rk, 2), 9), (1024,), 0, 1000, jnp.int32), jax.random.randint(jax.random.fold_in(jax.random.fold_in(_rk, 2), 10), (1024,), 2, 999, jnp.int32), jax.random.randint(jax.random.fold_in(jax.random.fold_in(_rk, 2), 11), (1024,), 0, 1000, jnp.int32), jax.random.randint(jax.random.fold_in(jax.random.fold_in(_rk, 2), 12), (1024,), 1, 1000, jnp.int32), jax.random.randint(jax.random.fold_in(jax.random.fold_in(_rk, 2), 13), (1024,), 0, 1000, jnp.int32), jax.random.randint(jax.random.fold_in(jax.random.fold_in(_rk, 2), 14), (1024,), 1, 1000, jnp.int32), jax.random.randint(jax.random.fold_in(jax.random.fold_in(_rk, 2), 15), (1024,), 1, 1000, jnp.int32), jax.random.randint(jax.random.fold_in(jax.random.fold_in(_rk, 2), 16), (1024,), 1, 1000, jnp.int32), jax.random.randint(jax.random.fold_in(jax.random.fold_in(_rk, 2), 17), (1024,), 9, 1000, jnp.int32), jax.random.randint(jax.random.fold_in(jax.random.fold_in(_rk, 2), 18), (1024,), 2, 1000, jnp.int32), jax.random.randint(jax.random.fold_in(jax.random.fold_in(_rk, 2), 19), (1024,), 4, 1000, jnp.int32), jax.random.randint(jax.random.fold_in(jax.random.fold_in(_rk, 2), 20), (1024,), 0, 7999, jnp.int32), jax.random.randint(jax.random.fold_in(jax.random.fold_in(_rk, 2), 21), (1024,), 6, 1000, jnp.int32), jax.random.randint(jax.random.fold_in(jax.random.fold_in(_rk, 2), 22), (1024,), 0, 1000, jnp.int32), jax.random.randint(jax.random.fold_in(jax.random.fold_in(_rk, 2), 23), (1024,), 2, 7997, jnp.int32), jax.random.randint(jax.random.fold_in(jax.random.fold_in(_rk, 2), 24), (1024,), 3, 7999, jnp.int32), jax.random.randint(jax.random.fold_in(jax.random.fold_in(_rk, 2), 25), (1024,), 0, 7997, jnp.int32)], axis=1)
        return (r_X_dense, r_X_sparse)
    r_X_dense, r_X_sparse = _rec_inputs()

    def _L0_rec_setup():
        import jax, jax.numpy as jnp
        import numpy as np
        F = 26
        V_FIELD = 1000
        V = F * V_FIELD
        D_EMB = 16
        DNN_IN = F * F * D_EMB
        H1, H2 = (256, 128)
        BS = 512
        NUM_DENSE = 13
        EPS = 1e-05

        def _bn(x, g, b):
            m = jnp.mean(x, axis=0)
            v = jnp.var(x, axis=0)
            return (x - m) * jax.lax.rsqrt(v + EPS) * g + b
        key = jax.random.key(seed)
        ks = jax.random.split(key, 16)

        def n(k, shape, s=0.05):
            return jax.random.normal(k, shape, dtype=jnp.float32) * s
        return {'X_sparse': jax.random.randint(ks[0], (BS, F), 0, V_FIELD, dtype=jnp.int32), 'X_dense': jax.random.normal(ks[1], (BS, NUM_DENSE), dtype=jnp.float32), 'fm1_emb': n(ks[2], (V, 1)), 'bias': jnp.zeros((1,), jnp.float32), 'fm1_dense_W': n(ks[3], (1, NUM_DENSE)), 'fm1_dense_b': jnp.zeros((1,), jnp.float32), 'emb_tables': n(ks[4], (F, V, D_EMB)), 'dense_W': n(ks[5], (DNN_IN, NUM_DENSE)), 'dense_b': jnp.zeros((DNN_IN,), jnp.float32), 'W1': n(ks[6], (H1, DNN_IN)), 'b1': jnp.zeros((H1,), jnp.float32), 'g1': jnp.ones((H1,), jnp.float32), 'beta1': jnp.zeros((H1,), jnp.float32), 'W2': n(ks[7], (H2, H1)), 'b2': jnp.zeros((H2,), jnp.float32), 'g2': jnp.ones((H2,), jnp.float32), 'beta2': jnp.zeros((H2,), jnp.float32), 'Wout': n(ks[8], (1, H2)), 'bout': jnp.zeros((1,), jnp.float32)}
    _L0_rec_all = _L0_rec_setup()
    _L0_rec_in = {k: v for k, v in _L0_rec_all.items() if k in ('fm1_emb', 'bias', 'fm1_dense_W', 'fm1_dense_b', 'emb_tables', 'dense_W', 'dense_b', 'W1', 'b1', 'g1', 'beta1', 'W2', 'b2', 'g2', 'beta2', 'Wout', 'bout')}
    del _L0_rec_all
    return {'r_X_dense': r_X_dense, 'r_X_sparse': r_X_sparse, 'L0_rec_fm1_emb': _L0_rec_in['fm1_emb'], 'L0_rec_bias': _L0_rec_in['bias'], 'L0_rec_fm1_dense_W': _L0_rec_in['fm1_dense_W'], 'L0_rec_fm1_dense_b': _L0_rec_in['fm1_dense_b'], 'L0_rec_emb_tables': _L0_rec_in['emb_tables'], 'L0_rec_dense_W': _L0_rec_in['dense_W'], 'L0_rec_dense_b': _L0_rec_in['dense_b'], 'L0_rec_W1': _L0_rec_in['W1'], 'L0_rec_b1': _L0_rec_in['b1'], 'L0_rec_g1': _L0_rec_in['g1'], 'L0_rec_beta1': _L0_rec_in['beta1'], 'L0_rec_W2': _L0_rec_in['W2'], 'L0_rec_b2': _L0_rec_in['b2'], 'L0_rec_g2': _L0_rec_in['g2'], 'L0_rec_beta2': _L0_rec_in['beta2'], 'L0_rec_Wout': _L0_rec_in['Wout'], 'L0_rec_bout': _L0_rec_in['bout']}

def reference(r_X_dense, r_X_sparse, L0_rec_fm1_emb, L0_rec_bias, L0_rec_fm1_dense_W, L0_rec_fm1_dense_b, L0_rec_emb_tables, L0_rec_dense_W, L0_rec_dense_b, L0_rec_W1, L0_rec_b1, L0_rec_g1, L0_rec_beta1, L0_rec_W2, L0_rec_b2, L0_rec_g2, L0_rec_beta2, L0_rec_Wout, L0_rec_bout):
    import jax
    import jax.numpy as jnp

    def _L0_rec_ref(X_sparse, X_dense, fm1_emb, bias, fm1_dense_W, fm1_dense_b, emb_tables, dense_W, dense_b, W1, b1, g1, beta1, W2, b2, g2, beta2, Wout, bout):
        import jax, jax.numpy as jnp
        import numpy as np
        F = 26
        V_FIELD = 1000
        V = F * V_FIELD
        D_EMB = 16
        DNN_IN = F * F * D_EMB
        H1, H2 = (256, 128)
        BS = 512
        NUM_DENSE = 13
        EPS = 1e-05

        def _bn(x, g, b):
            m = jnp.mean(x, axis=0)
            v = jnp.var(x, axis=0)
            return (x - m) * jax.lax.rsqrt(v + EPS) * g + b
        offsets = (jnp.arange(F, dtype=X_sparse.dtype) * V_FIELD)[None, :]
        X = X_sparse + offsets
        fm1 = jnp.sum(fm1_emb[X], axis=1) + bias
        fm1 = fm1 + X_dense @ fm1_dense_W.T + fm1_dense_b
        E = emb_tables[:, X, :]
        A = jnp.transpose(E, (1, 0, 2, 3))
        P = A * jnp.swapaxes(A, 1, 2)
        mask = jnp.triu(jnp.ones((F, F), jnp.float32), 1)
        fm2 = jnp.einsum('bijd,ij->b', P, mask)[:, None]
        dnn = A.reshape(A.shape[0], DNN_IN)
        dnn = dnn + jax.nn.relu(X_dense @ dense_W.T + dense_b)
        h = jax.nn.relu(_bn(dnn @ W1.T + b1, g1, beta1))
        h = jax.nn.relu(_bn(h @ W2.T + b2, g2, beta2))
        out = h @ Wout.T + bout
        return jax.nn.sigmoid(fm1 + fm2 + out)
    y = _L0_rec_ref(r_X_sparse, r_X_dense, L0_rec_fm1_emb, L0_rec_bias, L0_rec_fm1_dense_W, L0_rec_fm1_dense_b, L0_rec_emb_tables, L0_rec_dense_W, L0_rec_dense_b, L0_rec_W1, L0_rec_b1, L0_rec_g1, L0_rec_beta1, L0_rec_W2, L0_rec_b2, L0_rec_g2, L0_rec_beta2, L0_rec_Wout, L0_rec_bout)
    return y

_drawn_inputs = setup_inputs


def setup_inputs(seed=0):
    import zlib

    import numpy as np

    out = dict(_drawn_inputs(seed))
    spreads = {'L0_rec_dense_b': (0.0, 0.1),
     'L0_rec_b1': (0.0, 0.8),
     'L0_rec_g1': (1.0, 0.2),
     'L0_rec_beta1': (0.0, 0.588),
     'L0_rec_b2': (0.0, 0.8),
     'L0_rec_g2': (1.0, 0.581),
     'L0_rec_beta2': (0.0, 0.669)}
    factors = {}
    for name, (base, spread) in spreads.items():
        noise = np.random.default_rng([zlib.crc32(name.encode()), seed]).standard_normal(out[name].shape)
        drawn = base * np.exp(spread * noise) if base else spread * noise
        out[name] = jnp.asarray(drawn.astype(out[name].dtype))
    for name, factor in factors.items():
        out[name] = (out[name] * factor).astype(out[name].dtype)
    return out
```

```python
import concourse.bass as bass
from concourse import mybir
from contextlib import ExitStack

P = 128
B = 1024
NBT = B // P
HALF = NBT // 2
HB = B // 2
F = 26
V = F * 1000
D_EMB = 16
ROW = F * D_EMB
TROW = ROW + 1
K1 = F * ROW
H1, H2 = 256, 128
NHT = H1 // P
NDENSE = 13
DR = NDENSE + 1
EPS = 1e-5
NKT = -(-K1 // P)
NU = 2 * NKT
PARTS = 3
SPLIT_K = PARTS * PARTS * DR
FM1_COL = K1
X_COL = K1 + 8
DXW = X_COL + B
DXP = 8
DXC = DXW // DXP
SQ = F // 2
NA, NX, NXT, NWRAW, NW = 3, 4, 4, 3, 4
KPC = 2
NCH = -(-NKT // KPC)
R_AHEAD, T_AHEAD = 4, 2
W_AHEAD = 10
D_FIRST = 8 * P
PIECES = 37
C_B1, C_G1, C_BETA1, C_B2, C_G2, C_BETA2, C_WOUT, C_BIAS, C_BOUT, NPAR = 0, 2, 4, 6, 7, 8, 9, 10, 11, 12


def segments(kt):
    k, end, out = kt * P, min((kt + 1) * P, K1), []
    while k < end:
        f, c = divmod(k, ROW)
        n = min(end - k, ROW - c)
        out.append((f, c, k - kt * P, n))
        k += n
    return out


def width(kt):
    return min(P, K1 - kt * P)


def first_unit(f):
    return 2 * (f * ROW // P)


def last_unit(f):
    return 2 * (((f + 1) * ROW - 1) // P) + 1


def fm2_rows(v):
    out = []
    for f in range(1, F):
        a = first_unit(f)
        b = first_unit(f + 1) if f + 1 < F else NU
        if a <= v < b:
            n = b - a
            out += [(f, t) for t in range(NBT * (v - a) // n, NBT * (v - a + 1) // n)]
    return out


def fm2_count(f, t):
    return (f - 1) * NBT + t + 1


def keeps_at(v):
    out = []
    if v == 2:
        out += [(0, 0), (0, 1)]
    for f, t in fm2_rows(v - 1):
        if t % HALF == HALF - 1:
            out.append((f, t // HALF))
    return out


def recommender(nc, table, w1t, dx, xs, offs, params, w2t, parts, out):
    f32, f32r, bf16, i32 = mybir.dt.float32, mybir.dt.float32r, mybir.dt.bfloat16, mybir.dt.int32
    ALU = mybir.AluOpType
    ACT = mybir.ActivationFunctionType
    AX = mybir.AxisListType

    ctx = ExitStack()
    with ctx:
        def sb(name, shape, dt):
            return ctx.enter_context(nc.sbuf_tensor(name, shape, dt))

        def pb(name, shape, dt):
            return ctx.enter_context(nc.psum_tensor(name, shape, dt))

        def sem(name):
            return ctx.enter_context(nc.semaphore(name))

        gath = sb("gath", [P, NA, NBT, TROW], f32)
        kept = sb("kept", [P, NBT, SQ, SQ, D_EMB], f32)
        x = sb("x", [P, NX, HALF, P], f32)
        xhi = sb("xhi", [P, NXT, HB], f32r)
        xlo = sb("xlo", [P, NXT, HB], f32r)
        wraw = sb("wraw", [P, NWRAW, KPC * H1], f32)
        whi = sb("whi", [P, NW, KPC * H1], f32r)
        wlo = sb("wlo", [P, NW, KPC * H1], f32r)
        dense = sb("dense", [P, X_COL], bf16)
        xd = sb("xd", [P, B], bf16)
        prod = sb("prod", [P, 2, SQ * D_EMB], f32)
        fm2 = sb("fm2", [P, NBT, PIECES], f32)
        fm1 = sb("fm1", [P, F, NBT], f32)
        idx = sb("idx", [P, F, NBT], i32)
        par = sb("par", [P, NPAR], f32)
        w2 = sb("w2", [P, NHT, H2], f32)
        ident = sb("ident", [P, P], f32)
        stats = sb("stats", [P, NHT + 1, 2, 6], f32)
        mv = sb("mv", [P, NHT + 1, 2], f32)
        bn = sb("bn", [P, 8, NHT + 1], f32)
        fin = sb("fin", [P, 6, NBT], f32)

        kept_flat = kept[:].rearrange("p a b c d -> p (a b c d)")
        dxs = kept_flat[:, 0:DXC]
        rest = kept_flat[:, 2048:2048 + DXC]
        rest2 = kept_flat[:, 4096:4096 + DXC]
        part = [kept_flat[:, (6 + j) * 1024:(7 + j) * 1024].bitcast(bf16)[:, 0:DXC] for j in range(PARTS)]
        xi = kept_flat[:, 9216:9216 + F * NBT].bitcast(i32)
        of = kept_flat[:, 9472:9472 + F * NBT].bitcast(i32)
        xf = kept_flat[:, 9728:9728 + F * NBT]
        neg = kept_flat[:, 9984:9984 + F * NBT]
        hpre = kept_flat[:, 0:NHT * B].rearrange("p (t b) -> p t b", t=NHT)
        h1 = kept_flat[:, 2048:2048 + NHT * B].rearrange("p (t b) -> p t b", t=NHT)
        h2pre = kept_flat[:, 4096:4096 + B]
        h2 = kept_flat[:, 5120:5120 + B]

        acc = [[pb(f"acc{t}{g}", [P, HB], f32) for g in range(2)] for t in range(NHT)]
        rps = [pb(f"rps{i}", [P, HALF, P], f32) for i in range(2)]
        tps = [pb(f"tps{i}", [P, HB], f32) for i in range(2)]

        dx_in, xs_in, par_in = sem("dx_in"), sem("xs_in"), sem("par_in")
        idx_ready, part_ready, parts_out = sem("idx_ready"), sem("part_ready"), sem("parts_out")
        xd_in, dense_in, dense_rest_in = sem("xd_in"), sem("dense_in"), sem("dense_rest_in")
        w_in = [sem(f"w_in{i}") for i in range(NWRAW)]
        gathered = [sem(f"gathered{i}") for i in range(NA)]
        ident0, ident_ready = sem("ident0"), sem("ident_ready")
        r_done, x_done, t_done, hi_done, lo_done, mm_done = (
            sem(n) for n in ("r_done", "x_done", "t_done", "hi_done", "lo_done", "mm_done"))
        whi_done, wlo_done = sem("whi_done"), sem("wlo_done")
        fm2_done, prod_done, keep_done, fm1_done = sem("fm2_done"), sem("prod_done"), sem("keep_done"), sem("fm1_done")
        pre_done, step_done, hpre_done = sem("pre_done"), sem("step_done"), sem("hpre_done")
        std_done, h1_done, l2_done, h2pre_done, h2_done, logit_done = (
            sem(n) for n in ("std_done", "h1_done", "l2_done", "h2pre_done", "h2_done", "logit_done"))
        var_done, norm_done, sum_done, y_done, y_out = (
            sem(n) for n in ("var_done", "norm_done", "sum_done", "y_done", "y_out"))
        block = ctx.enter_context(nc.Block())

        def keep_count(f):
            return 2 * (f + 1)

        @block.sync
        def _(sp):
            sp.dma_start(xi, xs).then_inc(xs_in, 16)
            sp.dma_start(of, offs).then_inc(xs_in, 16)
            sp.dma_start(dxs[0:DR * DXP, :], dx).then_inc(dx_in, 16)
            for c in range(NWRAW):
                sp.dma_start(wraw[:, c, :], w1t[c]).then_inc(w_in[c], 16)
            sp.dma_start(par[:], params).then_inc(par_in, 16)
            sp.dma_start(w2[:], w2t).then_inc(par_in, 16)
            for j in range(PARTS):
                sp.wait_ge(part_ready, j + 1)
                sp.dma_start(parts[j].rearrange("r (g c) -> (r g) c", g=DXP), part[j][0:DR * DXP, :]).then_inc(parts_out, 16)
            sp.wait_ge(parts_out, 16 * PARTS)
            for i in range(PARTS):
                for j in range(PARTS):
                    at = (i * PARTS + j) * DR
                    sp.dma_start(xd[at:at + DR, :], parts[i, :, X_COL:DXW]).then_inc(xd_in, 16)
            rows = parts.rearrange("j r c -> (j r) c")
            for first, last, done in ((0, D_FIRST, dense_in), (D_FIRST, X_COL, dense_rest_in)):
                for i in range(PARTS):
                    at = i * PARTS * DR
                    sp.dma_start(dense[at:at + PARTS * DR, first:last], rows[:, first:last]).then_inc(done, 16)
            for c in range(NWRAW, NCH):
                sp.wait_ge(wlo_done, c - NWRAW + 1)
                sp.dma_start(wraw[:, c % NWRAW, :], w1t[c]).then_inc(w_in[c % NWRAW], 16)
            sp.wait_ge(y_done, 1)
            sp.dma_start(out, fin[:, 5, :]).then_inc(y_out, 16)
            sp.wait_ge(y_out, 16)

        @block.gpsimd
        def _(pool):
            nc.gpsimd.memset(ident[:], 0.0).then_inc(ident0, 1)
            pool.wait_ge(ident0, 1)
            nc.gpsimd.affine_select(out=ident[:], in_=ident[:], compare_op=ALU.not_equal, fill=1.0, base=0,
                                    pattern=[[-1, P]], channel_multiplier=1).then_inc(ident_ready, 1)
            chunk = 0
            pool.wait_ge(idx_ready, 1)
            for f in range(F + NA):
                while chunk < NCH and (f >= F or KPC * 2 * chunk <= f * 2 * ROW // P - 5):
                    if chunk >= NW:
                        pool.wait_ge(mm_done, 2 * KPC * (chunk - NW + 1))
                    pool.wait_ge(whi_done, chunk + 1)
                    nc.gpsimd.tensor_tensor(wlo[:, chunk % NW, :], wraw[:, chunk % NWRAW, :],
                                            whi[:, chunk % NW, :].bitcast(f32), ALU.subtract).then_inc(wlo_done, 1)
                    chunk += 1
                if f >= NA:
                    old = f - NA
                    pool.wait_ge(x_done, last_unit(old) + 1)
                    pool.wait_ge(keep_done, keep_count(old))
                    nc.gpsimd.tensor_copy(fm1[:, old, :], gath[:, old % NA, :, ROW]).then_inc(fm1_done, 1)
                if f < F:
                    if f >= NA:
                        pool.wait_ge(fm1_done, f - NA + 1)
                    for t in range(NBT):
                        nc.gpsimd.indirect_dma_start(
                            gath[:, f % NA, t, :], None, table,
                            bass.IndirectOffsetOnAxis(ap=idx[:, f, t:t + 1], axis=0)).then_inc(gathered[f % NA], 16)

        @block.scalar
        def _(act):
            def make_whi(c):
                act.wait_ge(w_in[c % NWRAW], 16 * (c // NWRAW + 1))
                if c >= NW:
                    act.wait_ge(mm_done, 2 * KPC * (c - NW + 1))
                nc.scalar.copy(whi[:, c % NW, :], wraw[:, c % NWRAW, :]).then_inc(whi_done, 1)

            def keep(f, g):
                tiles = slice(g * HALF, (g + 1) * HALF)
                src = gath[:, f % NA, tiles, 0:ROW].rearrange("p b (t d) -> p b t d", d=D_EMB)
                if f >= 1:
                    act.wait_ge(fm2_done, fm2_count(f, g * HALF + HALF - 1))
                if f == 0:
                    act.wait_ge(gathered[0], 16 * NBT)
                    act.wait_ge(parts_out, 16 * PARTS)
                    act.wait_ge(idx_ready, 1)
                if f < SQ:
                    last = nc.scalar.copy(kept[:, tiles, f, :, :], src[:, :, SQ:F, :])
                    if f + 1 < SQ:
                        last = nc.scalar.copy(kept[:, tiles, f + 1:SQ, f, :], src[:, :, f + 1:SQ, :])
                elif f + 1 < F:
                    c = f - SQ
                    last = nc.scalar.copy(kept[:, tiles, c + 1:SQ, c, :], src[:, :, f + 1:F, :])
                else:
                    last = act.nop()
                last.then_inc(keep_done, 1)

            chunk = 0
            for s in range(-R_AHEAD, NU):
                while chunk < NCH and 2 * KPC * chunk - W_AHEAD <= s:
                    make_whi(chunk)
                    chunk += 1
                u = s + T_AHEAD
                if 0 <= u < NU:
                    w = width(u // 2)
                    act.wait_ge(t_done, u + 1)
                    if u >= NXT:
                        act.wait_ge(mm_done, u - NXT + 1)
                    nc.scalar.copy(xhi[0:w, u % NXT, :], tps[u % 2][0:w, :]).then_inc(hi_done, 1)
                for f, g in keeps_at(s + R_AHEAD):
                    keep(f, g)

            act.wait_ge(par_in, 32)
            act.wait_ge(fm2_done, fm2_count(F - 1, NBT - 1))
            for g in range(2):
                act.wait_ge(mm_done, NU - 1 + g)
                for t in range(NHT):
                    nc.scalar.activation(hpre[:, t, g * HB:(g + 1) * HB], acc[t][g][:], ACT.Identity,
                                         bias=par[:, C_B1 + t:C_B1 + t + 1]).then_inc(hpre_done, 1)
            act.wait_ge(var_done, 1)
            nc.scalar.activation(bn[:, 1, 0:NHT], bn[:, 0, 0:NHT], ACT.Sqrt).then_inc(std_done, 1)
            act.wait_ge(norm_done, 1)
            for t in range(NHT):
                nc.scalar.activation(h1[:, t, :], hpre[:, t, :], ACT.Relu, bias=bn[:, 6, t:t + 1],
                                     scale=bn[:, 5, t:t + 1]).then_inc(h1_done, 1)
            act.wait_ge(l2_done, 1)
            for g in range(2):
                nc.scalar.activation(h2pre[:, g * HB:(g + 1) * HB], rps[g][:].rearrange("p a b -> p (a b)"),
                                     ACT.Identity, bias=par[:, C_B2:C_B2 + 1]).then_inc(h2pre_done, 1)
            act.wait_ge(var_done, 2)
            nc.scalar.activation(bn[:, 1, NHT:NHT + 1], bn[:, 0, NHT:NHT + 1], ACT.Sqrt).then_inc(std_done, 1)
            act.wait_ge(norm_done, 2)
            nc.scalar.activation(h2, h2pre, ACT.Relu, bias=bn[:, 6, NHT:NHT + 1],
                                 scale=bn[:, 5, NHT:NHT + 1]).then_inc(h2_done, 1)
            act.wait_ge(sum_done, 1)
            nc.scalar.activation(fin[:, 5, :], fin[:, 4, :], ACT.Sigmoid).then_inc(y_done, 1)

        @block.vector
        def _(dve):
            steps = [0]

            def link(ins):
                steps[0] += 1
                ins.then_inc(step_done, 1)
                dve.wait_ge(step_done, steps[0])

            dve.wait_ge(xs_in, 32)
            link(nc.vector.tensor_tensor(xf, xi, of, ALU.add))
            link(nc.vector.tensor_scalar(neg, xf, 0.0, float(V), ALU.is_lt, ALU.mult))
            link(nc.vector.tensor_tensor(xf, xf, neg, ALU.add))
            nc.vector.tensor_scalar(idx[:].rearrange("p f t -> p (f t)"), xf, 0.0, float(V - 1), ALU.max,
                                    ALU.min).then_inc(idx_ready, 1)
            dve.wait_ge(dx_in, 16)
            n = DR * DXP
            src = dxs
            for j, nxt in enumerate((rest, rest2, None)):
                nc.vector.tensor_copy(part[j][0:n, :], src[0:n, :]).then_inc(part_ready, 1)
                if nxt is not None:
                    dve.wait_ge(part_ready, j + 1)
                    link(nc.vector.tensor_tensor(nxt[0:n, :], src[0:n, :], part[j][0:n, :], ALU.subtract))
                    src = nxt

            products = [0]

            def product(f, t, piece, a, b):
                i = products[0]
                products[0] += 1
                if i >= 2:
                    dve.wait_ge(prod_done, i - 1)
                o = prod[:, i % 2, 0:a.shape[1] * D_EMB].rearrange("p (n d) -> p n d", d=D_EMB)
                nc.vector.scalar_tensor_tensor(out=o, in0=a, scalar=1.0, in1=b, op0=ALU.mult, op1=ALU.mult,
                                               accum_out=fm2[:, t, piece:piece + 1]).then_inc(prod_done, 1)
                return i + 1

            def interact(f, t):
                a = gath[:, f % NA, t, 0:ROW].rearrange("p (t d) -> p t d", d=D_EMB)
                dve.wait_ge(keep_done, keep_count(f - 1) - 1 + t // HALF)
                if f < SQ:
                    product(f, t, f - 1, a[:, 0:f, :], kept[:, t, f, 0:f, :])
                else:
                    c = f - SQ
                    piece = SQ - 1 + (2 * c - 1 if c else 0)
                    product(f, t, piece, a[:, 0:SQ, :], kept[:, t, 0:SQ, c, :])
                    if c:
                        product(f, t, piece + 1, a[:, SQ:f, :], kept[:, t, c, 0:c, :])
                dve.wait_ge(prod_done, products[0])
                dve.sem_inc(fm2_done, 1)

            for s in range(-R_AHEAD, NU):
                u = s + R_AHEAD
                if u < NU:
                    kt, g = divmod(u, 2)
                    dve.wait_ge(r_done, u + 1)
                    if u >= NX:
                        dve.wait_ge(t_done, u - NX + 1)
                    for f, c, o, n in segments(kt):
                        dve.wait_ge(gathered[f % NA], 16 * NBT * (f // NA + 1))
                        last = nc.vector.scalar_tensor_tensor(
                            out=x[:, u % NX, :, o:o + n], in0=rps[u % 2][:, :, o:o + n], scalar=0.0,
                            in1=gath[:, f % NA, g * HALF:(g + 1) * HALF, c:c + n], op0=ALU.max, op1=ALU.add)
                    last.then_inc(x_done, 1)
                    for f, t in fm2_rows(u):
                        interact(f, t)
                u = s + T_AHEAD
                if 0 <= u < NU:
                    w = width(u // 2)
                    dve.wait_ge(hi_done, u + 1)
                    nc.vector.tensor_tensor(xlo[0:w, u % NXT, :], tps[u % 2][0:w, :],
                                            xhi[0:w, u % NXT, :].bitcast(f32), ALU.subtract).then_inc(lo_done, 1)

            def normalise(first, n, g, beta):
                c = slice(first, first + n)
                mean, var = mv[:, c, 0], mv[:, c, 1]
                nc.vector.tensor_scalar_add(bn[:, 0, c], var, EPS).then_inc(var_done, 1)
                dve.wait_ge(std_done, 1 if first == 0 else 2)
                link(nc.vector.reciprocal(bn[:, 2, c], bn[:, 1, c]))
                link(nc.vector.tensor_tensor(bn[:, 3, c], bn[:, 2, c], bn[:, 2, c], ALU.mult))
                link(nc.vector.tensor_tensor(bn[:, 4, c], bn[:, 3, c], bn[:, 0, c], ALU.mult))
                link(nc.vector.tensor_scalar(bn[:, 3, c], bn[:, 4, c], -0.5, 1.5, ALU.mult, ALU.add))
                link(nc.vector.tensor_tensor(bn[:, 4, c], bn[:, 3, c], bn[:, 2, c], ALU.mult))
                link(nc.vector.tensor_tensor(bn[:, 5, c], bn[:, 4, c], par[:, g:g + n], ALU.mult))
                link(nc.vector.tensor_tensor(bn[:, 7, c], mean, bn[:, 5, c], ALU.mult))
                nc.vector.tensor_tensor(bn[:, 6, c], par[:, beta:beta + n], bn[:, 7, c],
                                        ALU.subtract).then_inc(norm_done, 1)

            dve.wait_ge(par_in, 32)
            for g in range(2):
                for t in range(NHT):
                    dve.wait_ge(hpre_done, g * NHT + t + 1)
                    last = nc.vector.bn_stats(stats[:, t, g, :], hpre[:, t, g * HB:(g + 1) * HB])
            link(last)
            for t in range(NHT):
                last = nc.vector.bn_aggr(mv[:, t, :], stats[:, t, :, :])
            link(last)
            normalise(0, NHT, C_G1, C_BETA1)
            dve.wait_ge(fm1_done, F)
            nc.vector.tensor_reduce(fin[:, 0, :], fm1[:].rearrange("p f t -> p t f"), AX.X, ALU.add)
            link(nc.vector.tensor_reduce(fin[:, 1, :], fm2[:], AX.X, ALU.add))
            link(nc.vector.tensor_tensor(fin[:, 2, :], fin[:, 0, :], fin[:, 1, :], ALU.add))
            link(nc.vector.tensor_scalar(fin[:, 3, :], fin[:, 2, :], par[:, C_BIAS:C_BIAS + 1],
                                         par[:, C_BOUT:C_BOUT + 1], ALU.add, ALU.add))
            for g in range(2):
                dve.wait_ge(h2pre_done, g + 1)
                last = nc.vector.bn_stats(stats[:, NHT, g, :], h2pre[:, g * HB:(g + 1) * HB])
            link(last)
            link(nc.vector.bn_aggr(mv[:, NHT, :], stats[:, NHT, :, :]))
            normalise(NHT, 1, C_G2, C_BETA2)
            dve.wait_ge(logit_done, 1)
            nc.vector.tensor_tensor(fin[:, 4, :], tps[0][:, 0:NBT], fin[:, 3, :], ALU.add).then_inc(sum_done, 1)

        @block.tensor
        def _(pe):
            def dense_products(u):
                kt, g = divmod(u, 2)
                w = width(kt)
                if u == 0:
                    pe.wait_ge(xd_in, 16 * PARTS * PARTS)
                    pe.wait_ge(dense_in, 16 * PARTS)
                if kt == D_FIRST // P and g == 0:
                    pe.wait_ge(dense_rest_in, 16 * PARTS)
                if u >= 2:
                    pe.wait_ge(x_done, u - 1)
                for q in range(HALF):
                    t = g * HALF + q
                    last = nc.tensor.matmul(rps[u % 2][:, q, 0:w], xd[0:SPLIT_K, t * P:(t + 1) * P],
                                            dense[0:SPLIT_K, kt * P:kt * P + w], start=True, stop=True)
                last.then_inc(r_done, 1)

            def transposes(u):
                w = width(u // 2)
                pe.wait_ge(x_done, u + 1)
                if u >= 2:
                    pe.wait_ge(lo_done, u - 1)
                for q in range(HALF):
                    last = nc.tensor.transpose(tps[u % 2][0:w, q * P:(q + 1) * P], x[:, u % NX, q, 0:w], ident[:])
                last.then_inc(t_done, 1)

            def layer1(u):
                kt, g = divmod(u, 2)
                w = width(kt)
                c = kt // KPC
                if u % (2 * KPC) == 0:
                    pe.wait_ge(wlo_done, c + 1)
                pe.wait_ge(lo_done, u + 1)
                for t in range(NHT):
                    col = kt % KPC * H1 + t * P
                    hi, lo = whi[0:w, c % NW, col:col + P], wlo[0:w, c % NW, col:col + P]
                    nc.tensor.matmul(acc[t][g][:], hi, xhi[0:w, u % NXT, :], start=(kt == 0), stop=False)
                    nc.tensor.matmul(acc[t][g][:], hi, xlo[0:w, u % NXT, :], start=False, stop=False)
                    last = nc.tensor.matmul(acc[t][g][:], lo, xhi[0:w, u % NXT, :], start=False,
                                            stop=(kt == NKT - 1))
                last.then_inc(mm_done, 1)

            pe.wait_ge(ident_ready, 1)
            for s in range(-R_AHEAD, NU):
                if s + R_AHEAD < NU:
                    dense_products(s + R_AHEAD)
                if 0 <= s + T_AHEAD < NU:
                    transposes(s + T_AHEAD)
                if s >= 0:
                    layer1(s)

            pe.wait_ge(par_in, 32)
            for t in range(NHT):
                pe.wait_ge(h1_done, t + 1)
                for g in range(2):
                    last = nc.tensor.matmul(rps[g][:].rearrange("p a b -> p (a b)"), w2[:, t, :],
                                            h1[:, t, g * HB:(g + 1) * HB], start=(t == 0), stop=(t == NHT - 1))
            last.then_inc(l2_done, 1)
            pe.wait_ge(h2_done, 1)
            for t in range(NBT):
                nc.tensor.matmul(tps[0][:, t:t + 1], xd[0:SPLIT_K, t * P:(t + 1) * P],
                                 dense[0:SPLIT_K, FM1_COL:FM1_COL + 1], start=True, stop=False)
                last = nc.tensor.matmul(tps[0][:, t:t + 1], h2[:, t * P:(t + 1) * P], par[:, C_WOUT:C_WOUT + 1],
                                        start=False, stop=True)
            last.then_inc(logit_done, 1)


def kernel(r_X_dense, r_X_sparse, L0_rec_fm1_emb, L0_rec_bias, L0_rec_fm1_dense_W, L0_rec_fm1_dense_b,
           L0_rec_emb_tables, L0_rec_dense_W, L0_rec_dense_b, L0_rec_W1, L0_rec_b1, L0_rec_g1, L0_rec_beta1,
           L0_rec_W2, L0_rec_b2, L0_rec_g2, L0_rec_beta2, L0_rec_Wout, L0_rec_bout):
    import numpy as np
    import concourse.bacc as bacc
    from concourse.bass_utils import run_bass_kernel_spmd

    def a(v):
        return np.asarray(v)

    def by_field(v):
        v = a(v)
        return v.reshape(F, F, D_EMB, -1).transpose(1, 0, 2, 3).reshape(K1, -1)

    table = np.concatenate([a(L0_rec_emb_tables).transpose(1, 0, 2).reshape(V, ROW), a(L0_rec_fm1_emb)], axis=1)
    w1 = np.zeros((NCH * KPC * P, H1), np.float32)
    w1[:K1] = by_field(a(L0_rec_W1).T)
    w1 = w1.reshape(NCH, KPC, P, H1).transpose(0, 2, 1, 3).reshape(NCH, P, KPC * H1)
    dx = np.zeros((DR, DXW), np.float32)
    dx[:NDENSE, :K1] = by_field(L0_rec_dense_W).T
    dx[NDENSE, :K1] = by_field(L0_rec_dense_b)[:, 0]
    dx[:NDENSE, FM1_COL] = a(L0_rec_fm1_dense_W)[0]
    dx[NDENSE, FM1_COL] = a(L0_rec_fm1_dense_b)[0]
    dx[:NDENSE, X_COL:] = a(r_X_dense).reshape(P, NBT, NDENSE).transpose(2, 1, 0).reshape(NDENSE, B)
    dx[NDENSE, X_COL:] = 1.0
    dx = dx.reshape(DR * DXP, DXC)
    xs = a(r_X_sparse).reshape(P, NBT, F).transpose(0, 2, 1).reshape(P, F * NBT)
    offs = np.broadcast_to((np.arange(F, dtype=np.int32) * (V // F))[None, :, None], (P, F, NBT)).reshape(P, F * NBT)
    params = np.zeros((P, NPAR), np.float32)
    params[:, C_B1:C_B1 + NHT] = a(L0_rec_b1).reshape(NHT, P).T
    params[:, C_G1:C_G1 + NHT] = a(L0_rec_g1).reshape(NHT, P).T
    params[:, C_BETA1:C_BETA1 + NHT] = a(L0_rec_beta1).reshape(NHT, P).T
    params[:, C_B2], params[:, C_G2], params[:, C_BETA2] = a(L0_rec_b2), a(L0_rec_g2), a(L0_rec_beta2)
    params[:, C_WOUT] = a(L0_rec_Wout)[0]
    params[:, C_BIAS] = a(L0_rec_bias)[0]
    params[:, C_BOUT] = a(L0_rec_bout)[0]
    w2 = a(L0_rec_W2).T.reshape(NHT, P, H2).transpose(1, 0, 2)

    nc = bacc.Bacc("TRN2", target_bir_lowering=False, num_devices=1)
    arrays, args = {}, []
    for name, v in (("table", table), ("w1t", w1), ("dx", dx), ("xs", xs), ("offs", offs), ("params", params), ("w2t", w2)):
        arrays[name] = np.ascontiguousarray(v)
        args.append(nc.dram_tensor(name, v.shape, mybir.dt.from_np(v.dtype), kind="ExternalInput").ap())
    parts = nc.dram_tensor("parts", (PARTS, DR, DXW), mybir.dt.bfloat16, kind="Internal").ap()
    out = nc.dram_tensor("y", (P, NBT), mybir.dt.float32, kind="ExternalOutput").ap()
    recommender(nc, *args, parts, out)
    r = run_bass_kernel_spmd(nc, [arrays], core_ids=[0])
    return np.asarray(r.results[0]["y"]).reshape(B, 1)
```

```python
import concourse.bass as bass
from concourse import mybir
from contextlib import ExitStack

P = 128
B = 1024
NBT = B // P
HALF = NBT // 2
NPAIR = NBT // 2
HB = B // 2
F = 26
V = F * 1000
D_EMB = 16
ROW = F * D_EMB
TROW = ROW + 1
K1 = F * ROW
H1, H2 = 256, 128
NHT = H1 // P
NDENSE = 13
DR = NDENSE + 1
EPS = 1e-5
NKT = -(-K1 // P)
NU = 2 * NKT
PARTS = 3
SPLIT_K = PARTS * PARTS * DR
FM1_COL = K1
DW = K1 + 8
DXP = 8
D_FIRST = 8 * P
D1C = (DW - D_FIRST) // DXP
D_MORE = 8 * P
SQ = F // 2
SPLITS = (("d", 0, 2 * P), ("x", 0, HB), ("x", HB, B), ("d", 2 * P, D_FIRST))
REST_REM = (-3, 0)
REST_PART = (-2, 0)
NA, NX, NXT, NWRAW, NW = 3, 4, 4, 4, 4
KPC = 2
NCH = -(-NKT // KPC)
R_AHEAD, T_AHEAD = 4, 2
W_AHEAD = 10
TURN = 2 * KPC * NW
SPLIT_WAITS = {0: 2, 1: 3, 4: 4}
H1_ACT, H1_DVE = ((0, 0), (0, 1), (1, 1)), ((1, 0),)
C_B1, C_G1, C_BETA1, C_B2, C_G2, C_BETA2, C_WOUT, C_BIAS, C_BOUT = 0, 2, 4, 6, 7, 8, 9, 10, 11
C_MASK, NPAR = 12, 16


def segments(kt):
    k, end, out = kt * P, min((kt + 1) * P, K1), []
    while k < end:
        f, c = divmod(k, ROW)
        n = min(end - k, ROW - c)
        out.append((f, c, k - kt * P, n))
        k += n
    return out


def width(kt):
    return min(P, K1 - kt * P)


def first_unit(f):
    return 2 * (f * ROW // P)


def last_unit(f):
    return 2 * (((f + 1) * ROW - 1) // P) + 1


def fm2_pairs(v):
    out = []
    for f in range(1, F):
        a = first_unit(f)
        b = first_unit(f + 1) if f + 1 < F else NU
        if a <= v < b:
            n = b - a
            out += [(f, t) for t in range(-(-NPAIR * (v - a) // n), -(-NPAIR * (v - a + 1) // n))]
    return out


def pair_count(f, t):
    return (f - 1) * NPAIR + t + 1


def keeps_at(v):
    out = []
    if v in (3, 4):
        out.append((0, v - 3))
    for f, t in fm2_pairs(v - 1):
        if (t + 1) * 2 % HALF == 0:
            out.append((f, (t + 1) * 2 // HALF - 1))
    return out


def recommender(nc, table, w1t, x0, d0, d1, xs, params, w2t, parts, out):
    f32, f32r, bf16, i32 = mybir.dt.float32, mybir.dt.float32r, mybir.dt.bfloat16, mybir.dt.int32
    ALU = mybir.AluOpType
    ACT = mybir.ActivationFunctionType
    AX = mybir.AxisListType

    ctx = ExitStack()
    with ctx:
        def sb(name, shape, dt):
            return ctx.enter_context(nc.sbuf_tensor(name, shape, dt))

        def pb(name, shape, dt):
            return ctx.enter_context(nc.psum_tensor(name, shape, dt))

        def sem(name):
            return ctx.enter_context(nc.semaphore(name))

        gath = sb("gath", [P, NA, NBT, TROW], f32)
        kept = sb("kept", [P, NBT, SQ, SQ, D_EMB], f32)
        x = sb("x", [P, NX, HALF, P], f32)
        xhi = sb("xhi", [P, NXT, HB], f32r)
        xlo = sb("xlo", [P, NXT, HB], f32r)
        wraw = sb("wraw", [P, NWRAW, KPC * H1], f32)
        whi = sb("whi", [P, NW, KPC * H1], f32r)
        wlo = sb("wlo", [P, NW, KPC * H1], f32r)
        dense = sb("dense", [P, DW], bf16)
        xd = sb("xd", [P, B], bf16)
        prod = sb("prod", [P, 2, 2, (F - 1) * D_EMB], f32)
        fm2 = sb("fm2", [P, NBT, F - 1], f32)
        fm1 = sb("fm1", [P, F, NBT], f32)
        idx = sb("idx", [P, F, NBT], i32)
        par = sb("par", [P, NPAR], f32)
        w2 = sb("w2", [P, NHT, H2], f32)
        ident = sb("ident", [P, P], f32)
        stats = sb("stats", [P, NHT + 1, 2, 6], f32)
        mv = sb("mv", [P, NHT + 1, 2], f32)
        bn = sb("bn", [P, 8, NHT + 1], f32)
        fin = sb("fin", [P, 6, NBT], f32)
        warm = sb("warm", [P, 3], f32)

        kept_flat = kept[:].rearrange("p a b c d -> p (a b c d)")
        def room(at, n):
            return kept_flat[:, at:at + n]

        raw = {"x": room(0, B), "d": room(1024, D_FIRST)}
        rem = {"x": room(2048, B), "d": room(3072, D_FIRST)}
        head = {"x": room(4096, B // 2).bitcast(bf16), "d": room(4608, D_FIRST // 2).bitcast(bf16)}
        mid = {"x": room(5120, B // 2).bitcast(bf16), "d": room(5632, D_FIRST // 2).bitcast(bf16)}
        part = dense[:, D_FIRST:D_FIRST + PARTS * D1C].rearrange("p (j c) -> p j c", j=PARTS)
        left_at = D_FIRST + (PARTS + 1) * D1C // 2 * 2
        left = dense[:, left_at:left_at + 2 * D1C].bitcast(f32)
        xi = room(14336, F * NBT).bitcast(i32)
        of = room(14592, F * NBT).bitcast(i32)
        xf = room(14848, F * NBT)
        neg = room(15104, F * NBT)
        h1 = room(0, NHT * B).rearrange("p (t b) -> p t b", t=NHT)
        h2 = room(2048, B)

        acc = [[pb(f"acc{t}{g}", [P, HB], f32) for g in range(2)] for t in range(NHT)]
        rps = [pb(f"rps{i}", [P, HALF, P], f32) for i in range(2)]
        tps = [pb(f"tps{i}", [P, HB], f32) for i in range(2)]

        x0_in, d0_in, d1_in, xs_in, par_in, par2_in = (
            sem(n) for n in ("x0_in", "d0_in", "d1_in", "xs_in", "par_in", "par2_in"))
        idx_ready, offs_ready, part_ready, rest_ready, parts_out = (
            sem(n) for n in ("idx_ready", "offs_ready", "part_ready", "rest_ready", "parts_out"))
        head_done, rem_done, mid_done, split_done = (
            sem(n) for n in ("head_done", "rem_done", "mid_done", "split_done"))
        dense_more_in, dense_rest_in = sem("dense_more_in"), sem("dense_rest_in")
        w_in = [sem(f"w_in{i}") for i in range(NWRAW)]
        gathered = [[sem(f"gathered{i}_{g}") for g in range(2)] for i in range(NA)]
        ident0, ident_ready = sem("ident0"), sem("ident_ready")
        r_done, x_done, t_done, hi_done, lo_done, mm_done = (
            sem(n) for n in ("r_done", "x_done", "t_done", "hi_done", "lo_done", "mm_done"))
        whi_done, wlo_done = sem("whi_done"), sem("wlo_done")
        prod_done, acc_done, keep_done, fm1_done = sem("prod_done"), sem("acc_done"), sem("keep_done"), sem("fm1_done")
        last_done = sem("last_done")
        step_done, warm_ready, std_done, l2_done, h2_done, logit_done = (
            sem(n) for n in ("step_done", "warm_ready", "std_done", "l2_done", "h2_done", "logit_done"))
        h1_done = [[sem(f"h1_done{t}{g}") for g in range(2)] for t in range(NHT)]
        var_done, norm_done, sum_done, y_done, y_out = (
            sem(n) for n in ("var_done", "norm_done", "sum_done", "y_done", "y_out"))
        block = ctx.enter_context(nc.Block())

        def keep_count(f):
            return 2 * (f + 1)

        @block.sync
        def _(sp):
            sp.dma_start(xi, xs).then_inc(xs_in, 16)
            sp.dma_start(raw["x"][0:SPLIT_K, :], x0).then_inc(x0_in, 16)
            for c in range(NWRAW):
                sp.dma_start(wraw[:, c, :], w1t[c]).then_inc(w_in[c], 16)
            sp.dma_start(w2[:], w2t).then_inc(par2_in, 16)

            def load_w(c):
                sp.wait_ge(wlo_done, c - NWRAW + 1)
                sp.dma_start(wraw[:, c % NWRAW, :], w1t[c]).then_inc(w_in[c % NWRAW], 16)

            load_w(NWRAW)
            sp.wait_ge(part_ready, PARTS)
            sp.dma_start(parts.rearrange("j r g c -> (r g) j c"), part[0:DR * DXP, :, :]).then_inc(parts_out, 16)
            sp.wait_ge(parts_out, 16)
            rows = parts.rearrange("j r g c -> (j r) (g c)")
            for a, b, done in ((0, D_MORE, dense_more_in), (D_MORE, DW - D_FIRST, dense_rest_in)):
                for i in range(PARTS):
                    at = i * PARTS * DR
                    sp.dma_start(dense[at:at + PARTS * DR, D_FIRST + a:D_FIRST + b], rows[:, a:b]).then_inc(done, 16)
                load_w(NWRAW + (1 if a == 0 else 2))
            first = NWRAW + 3
            turns = (NCH - first) // NWRAW
            with nc.sync.Fori(0, turns) as turn:
                base = turn * NWRAW
                for j in range(first, first + NWRAW):
                    sp.wait_ge(wlo_done, base + (j - NWRAW + 1))
                    sp.dma_start(wraw[:, j % NWRAW, :], w1t[bass.ds(base + j, 1)].rearrange("c p h -> p (c h)")).then_inc(
                        w_in[j % NWRAW], 16)
            for c in range(first + turns * NWRAW, NCH):
                load_w(c)
            sp.wait_ge(y_done, 1)
            sp.dma_start(out, fin[:, 5, :]).then_inc(y_out, 16)
            sp.wait_ge(y_out, 16)

        @block.gpsimd
        def _(pool):
            nc.gpsimd.iota(of, pattern=[[V // F, F], [0, NBT]], base=0, channel_multiplier=0).then_inc(offs_ready, 1)
            nc.gpsimd.memset(ident[:], 0.0).then_inc(ident0, 1)
            pool.wait_ge(ident0, 1)
            nc.gpsimd.affine_select(out=ident[:], in_=ident[:], compare_op=ALU.not_equal, fill=1.0, base=0,
                                    pattern=[[-1, P]], channel_multiplier=1).then_inc(ident_ready, 1)
            chunk = 0
            pool.wait_ge(idx_ready, 1)
            for f in range(F + NA):
                if f == 1:
                    pool.wait_ge(idx_ready, 2)
                while chunk < NCH and (f >= F or KPC * 2 * chunk <= f * 2 * ROW // P - 5):
                    if chunk >= NW:
                        pool.wait_ge(mm_done, 2 * KPC * (chunk - NW + 1))
                    pool.wait_ge(whi_done, chunk + 1)
                    nc.gpsimd.tensor_tensor(wlo[:, chunk % NW, :], wraw[:, chunk % NWRAW, :],
                                            whi[:, chunk % NW, :].bitcast(f32), ALU.subtract).then_inc(wlo_done, 1)
                    chunk += 1
                if f >= NA:
                    old = f - NA
                    pool.wait_ge(x_done, last_unit(old) + 1)
                    pool.wait_ge(keep_done, keep_count(old))
                    nc.gpsimd.tensor_copy(fm1[:, old, :], gath[:, old % NA, :, ROW]).then_inc(fm1_done, 1)
                if f < F:
                    if f >= NA:
                        pool.wait_ge(fm1_done, f - NA + 1)
                    for t in range(NBT):
                        nc.gpsimd.indirect_dma_start(
                            gath[:, f % NA, t, :], None, table,
                            bass.IndirectOffsetOnAxis(ap=idx[:, f, t:t + 1], axis=0)).then_inc(gathered[f % NA][t // HALF], 16)

        @block.scalar
        def _(act):
            def make_whi(c):
                act.wait_ge(w_in[c % NWRAW], 16 * (c // NWRAW + 1))
                if c >= NW:
                    act.wait_ge(mm_done, 2 * KPC * (c - NW + 1))
                nc.scalar.copy(whi[:, c % NW, :], wraw[:, c % NWRAW, :]).then_inc(whi_done, 1)

            def accumulate(f, t):
                act.wait_ge(prod_done, pair_count(f, t))
                for i in range(2):
                    row = prod[:, pair_count(f, t) % 2, i, 0:f * D_EMB]
                    last = nc.scalar.activation(row, row, ACT.Copy, accum_out=fm2[:, 2 * t + i, f - 1:f])
                last.then_inc(acc_done, 1)

            def keep(f, g):
                tiles = slice(g * HALF, (g + 1) * HALF)
                src = gath[:, f % NA, tiles, 0:ROW].rearrange("p b (t d) -> p b t d", d=D_EMB)
                if f >= 1:
                    act.wait_ge(prod_done, pair_count(f, (g + 1) * HALF // 2 - 1))
                if f == 0:
                    act.wait_ge(gathered[0][g], 16 * HALF)
                    act.wait_ge(split_done, len(SPLITS))
                    act.wait_ge(idx_ready, 2)
                if f < SQ:
                    last = nc.scalar.copy(kept[:, tiles, f, :, :], src[:, :, SQ:F, :])
                    if f + 1 < SQ:
                        last = nc.scalar.copy(kept[:, tiles, f + 1:SQ, f, :], src[:, :, f + 1:SQ, :])
                elif f + 1 < F:
                    c = f - SQ
                    last = nc.scalar.copy(kept[:, tiles, c + 1:SQ, c, :], src[:, :, f + 1:F, :])
                else:
                    last = act.nop()
                last.then_inc(keep_done, 1)

            act.dma_start(par[:], params).then_inc(par_in, 16)
            act.dma_start(raw["d"][0:SPLIT_K, :], d0).then_inc(d0_in, 16)
            act.dma_start(left[0:DR * DXP, :], d1).then_inc(d1_in, 16)
            act.wait_ge(warm_ready, 1)
            nc.scalar.activation(warm[:, 1:2], warm[:, 0:1], ACT.Sqrt)

            def split_head(n):
                of_, a, b = SPLITS[n]
                act.wait_ge(x0_in if of_ == "x" else d0_in, 16)
                nc.scalar.copy(head[of_][0:SPLIT_K, a:b], raw[of_][0:SPLIT_K, a:b]).then_inc(head_done, 1)

            def split_mid(n):
                of_, a, b = SPLITS[n]
                act.wait_ge(rem_done, n + 1)
                nc.scalar.copy(mid[of_][0:SPLIT_K, a:b], rem[of_][0:SPLIT_K, a:b]).then_inc(mid_done, 1)

            def rest_part(j):
                if j == 0:
                    act.wait_ge(d1_in, 16)
                else:
                    act.wait_ge(rest_ready, j)
                nc.scalar.copy(part[0:DR * DXP, j, :], left[0:DR * DXP, :]).then_inc(part_ready, 1)

            for n in range(len(SPLITS) + 1):
                if n < len(SPLITS):
                    split_head(n)
                if n >= 1:
                    split_mid(n - 1)
            make_whi(0)
            rest_part(0)
            make_whi(1)
            chunk = 2
            for s in range(-R_AHEAD, NU):
                while chunk < NCH and 2 * KPC * chunk - W_AHEAD <= s:
                    make_whi(chunk)
                    chunk += 1
                u = s + T_AHEAD
                if 0 <= u < NU:
                    w = width(u // 2)
                    act.wait_ge(t_done, u + 1)
                    if u >= NXT:
                        act.wait_ge(mm_done, u - NXT + 1)
                    nc.scalar.copy(xhi[0:w, u % NXT, :], tps[u % 2][0:w, :]).then_inc(hi_done, 1)
                if s in REST_PART:
                    rest_part(1 + REST_PART.index(s))
                for f, g in keeps_at(s + R_AHEAD):
                    keep(f, g)
                for f, t in fm2_pairs(s + R_AHEAD - 1):
                    accumulate(f, t)

            act.wait_ge(var_done, 1)
            nc.scalar.activation(bn[:, 1, 0:NHT], bn[:, 0, 0:NHT], ACT.Sqrt).then_inc(std_done, 1)
            act.wait_ge(norm_done, 1)
            act.wait_ge(prod_done, pair_count(F - 1, NPAIR - 1))
            for t, g in H1_ACT:
                nc.scalar.activation(h1[:, t, g * HB:(g + 1) * HB], acc[t][g][:], ACT.Relu, bias=bn[:, 6, t:t + 1],
                                     scale=bn[:, 5, t:t + 1]).then_inc(h1_done[t][g], 1)
            act.wait_ge(var_done, 2)
            nc.scalar.activation(bn[:, 1, NHT:NHT + 1], bn[:, 0, NHT:NHT + 1], ACT.Sqrt).then_inc(std_done, 1)
            nc.scalar.activation(warm[:, 2:3], warm[:, 0:1], ACT.Sigmoid)
            act.wait_ge(norm_done, 2)
            for g in range(2):
                nc.scalar.activation(h2[:, g * HB:(g + 1) * HB], rps[g][:].rearrange("p a b -> p (a b)"), ACT.Relu,
                                     bias=bn[:, 6, NHT:NHT + 1], scale=bn[:, 5, NHT:NHT + 1]).then_inc(h2_done, 1)
            act.wait_ge(sum_done, 1)
            nc.scalar.activation(fin[:, 5, :], fin[:, 4, :], ACT.Sigmoid).then_inc(y_done, 1)

        @block.vector
        def _(dve):
            steps = [0]

            def link(ins):
                steps[0] += 1
                ins.then_inc(step_done, 1)
                dve.wait_ge(step_done, steps[0])

            nc.vector.memset(warm[:, 0:1], 1.0).then_inc(warm_ready, 1)
            def split_rem(n):
                of_, a, b = SPLITS[n]
                m = C_MASK + (0 if of_ == "x" else 2)
                dve.wait_ge(head_done, n + 1)
                nc.vector.scalar_tensor_tensor(
                    out=rem[of_][0:SPLIT_K, a:b], in0=head[of_][0:SPLIT_K, a:b], scalar=par[0:SPLIT_K, m:m + 1],
                    in1=raw[of_][0:SPLIT_K, a:b], op0=ALU.mult, op1=ALU.add).then_inc(rem_done, 1)

            def split_last(n):
                of_, a, b = SPLITS[n]
                m = C_MASK + (1 if of_ == "x" else 3)
                dve.wait_ge(mid_done, n + 1)
                nc.vector.scalar_tensor_tensor(
                    out={"x": xd, "d": dense}[of_][0:SPLIT_K, a:b], in0=mid[of_][0:SPLIT_K, a:b],
                    scalar=par[0:SPLIT_K, m:m + 1], in1=rem[of_][0:SPLIT_K, a:b], op0=ALU.mult,
                    op1=ALU.add).then_inc(split_done, 1)

            def rest_rem(j):
                dve.wait_ge(part_ready, j + 1)
                rows = left[0:DR * DXP, :]
                nc.vector.tensor_tensor(rows, rows, part[0:DR * DXP, j, :], ALU.subtract).then_inc(rest_ready, 1)

            dve.wait_ge(xs_in, 16)
            dve.wait_ge(offs_ready, 1)
            for a, b in ((0, NBT), (NBT, F * NBT)):
                link(nc.vector.tensor_tensor(xf[:, a:b], xi[:, a:b], of[:, a:b], ALU.add))
                link(nc.vector.tensor_scalar(neg[:, a:b], xf[:, a:b], 0.0, float(V), ALU.is_lt, ALU.mult))
                link(nc.vector.tensor_tensor(xf[:, a:b], xf[:, a:b], neg[:, a:b], ALU.add))
                nc.vector.tensor_scalar(idx[:].rearrange("p f t -> p (f t)")[:, a:b], xf[:, a:b], 0.0, float(V - 1),
                                        ALU.max, ALU.min).then_inc(idx_ready, 1)
            dve.wait_ge(par_in, 16)
            for n in range(len(SPLITS) + 1):
                if n < len(SPLITS):
                    split_rem(n)
                if n >= 1:
                    split_last(n - 1)

            def multiply(f, t):
                tiles = slice(2 * t, 2 * t + 2)
                a = gath[:, f % NA, tiles, 0:ROW].rearrange("p b (t d) -> p b t d", d=D_EMB)
                dve.wait_ge(keep_done, keep_count(f - 1) - 1 + 2 * t // HALF)
                n = pair_count(f, t)
                if n > 2:
                    dve.wait_ge(acc_done, n - 2)
                o = prod[:, n % 2, :, 0:f * D_EMB].rearrange("p b (t d) -> p b t d", d=D_EMB)
                if f < SQ:
                    last = nc.vector.tensor_tensor(o, a[:, :, 0:f, :], kept[:, tiles, f, 0:f, :], ALU.mult)
                else:
                    c = f - SQ
                    last = nc.vector.tensor_tensor(o[:, :, 0:SQ, :], a[:, :, 0:SQ, :], kept[:, tiles, 0:SQ, c, :],
                                                   ALU.mult)
                    if c:
                        last = nc.vector.tensor_tensor(o[:, :, SQ:f, :], a[:, :, SQ:f, :],
                                                       kept[:, tiles, c, 0:c, :], ALU.mult)
                last.then_inc(prod_done, 1)

            for s in range(-R_AHEAD, NU):
                if s in REST_REM:
                    rest_rem(REST_REM.index(s))
                u = s + R_AHEAD
                if u < NU:
                    kt, g = divmod(u, 2)
                    dve.wait_ge(r_done, u + 1)
                    if u >= NX:
                        dve.wait_ge(t_done, u - NX + 1)
                    for f, c, o, n in segments(kt):
                        dve.wait_ge(gathered[f % NA][g], 16 * HALF * (f // NA + 1))
                        last = nc.vector.scalar_tensor_tensor(
                            out=x[:, u % NX, :, o:o + n], in0=rps[u % 2][:, :, o:o + n], scalar=0.0,
                            in1=gath[:, f % NA, g * HALF:(g + 1) * HALF, c:c + n], op0=ALU.max, op1=ALU.add)
                    last.then_inc(x_done, 1)
                    for f, t in fm2_pairs(u):
                        multiply(f, t)
                u = s + T_AHEAD
                if 0 <= u < NU:
                    w = width(u // 2)
                    dve.wait_ge(hi_done, u + 1)
                    nc.vector.tensor_tensor(xlo[0:w, u % NXT, :], tps[u % 2][0:w, :],
                                            xhi[0:w, u % NXT, :].bitcast(f32), ALU.subtract).then_inc(lo_done, 1)

            def normalise(first, n, bias, g, beta):
                c = slice(first, first + n)
                raw_mean, var = mv[:, c, 0], mv[:, c, 1]
                nc.vector.tensor_scalar_add(bn[:, 0, c], var, EPS).then_inc(var_done, 1)
                link(nc.vector.tensor_tensor(bn[:, 2, c], raw_mean, par[:, bias:bias + n], ALU.add))
                link(nc.vector.tensor_tensor(bn[:, 7, c], par[:, bias:bias + n], bn[:, 2, c], ALU.subtract))
                dve.wait_ge(std_done, 1 if first == 0 else 2)
                link(nc.vector.reciprocal(bn[:, 2, c], bn[:, 1, c]))
                nc.vector.tensor_tensor(bn[:, 1, c], bn[:, 2, c], par[:, g:g + n], ALU.mult)
                link(nc.vector.scalar_tensor_tensor(out=bn[:, 3, c], in0=bn[:, 2, c], scalar=-0.5, in1=bn[:, 2, c],
                                                    op0=ALU.mult, op1=ALU.mult))
                link(nc.vector.tensor_tensor(bn[:, 4, c], bn[:, 3, c], bn[:, 0, c], ALU.mult))
                link(nc.vector.scalar_tensor_tensor(out=bn[:, 5, c], in0=bn[:, 4, c], scalar=1.5, in1=bn[:, 1, c],
                                                    op0=ALU.add, op1=ALU.mult))
                link(nc.vector.tensor_tensor(bn[:, 3, c], bn[:, 7, c], bn[:, 5, c], ALU.mult))
                link(nc.vector.tensor_tensor(bn[:, 6, c], bn[:, 3, c], par[:, beta:beta + n], ALU.add))
                dve.sem_inc(norm_done, 1)

            for g in range(2):
                for t in range(NHT):
                    if g == 0:
                        dve.wait_ge(mm_done, NU - 1)
                    else:
                        dve.wait_ge(last_done, t + 1)
                    last = nc.vector.bn_stats(stats[:, t, g, :], acc[t][g][:])
            link(last)
            for t in range(NHT):
                last = nc.vector.bn_aggr(mv[:, t, :], stats[:, t, :, :])
            link(last)
            normalise(0, NHT, C_B1, C_G1, C_BETA1)
            for t, g in H1_DVE:
                o = h1[:, t, g * HB:(g + 1) * HB]
                link(nc.vector.tensor_scalar(o, acc[t][g][:], bn[:, 5, t:t + 1], bn[:, 6, t:t + 1], ALU.mult, ALU.add))
                nc.vector.tensor_scalar_max(o, o, 0.0).then_inc(h1_done[t][g], 1)
            dve.wait_ge(fm1_done, F)
            dve.wait_ge(acc_done, pair_count(F - 1, NPAIR - 1))
            nc.vector.tensor_reduce(fin[:, 0, :], fm1[:].rearrange("p f t -> p t f"), AX.X, ALU.add)
            link(nc.vector.tensor_reduce(fin[:, 1, :], fm2[:], AX.X, ALU.add))
            link(nc.vector.tensor_tensor(fin[:, 2, :], fin[:, 0, :], fin[:, 1, :], ALU.add))
            link(nc.vector.tensor_scalar(fin[:, 3, :], fin[:, 2, :], par[:, C_BIAS:C_BIAS + 1],
                                         par[:, C_BOUT:C_BOUT + 1], ALU.add, ALU.add))
            for g in range(2):
                dve.wait_ge(l2_done, g + 1)
                last = nc.vector.bn_stats(stats[:, NHT, g, :], rps[g][:].rearrange("p a b -> p (a b)"))
            link(last)
            link(nc.vector.bn_aggr(mv[:, NHT, :], stats[:, NHT, :, :]))
            normalise(NHT, 1, C_B2, C_G2, C_BETA2)
            dve.wait_ge(logit_done, 1)
            nc.vector.tensor_tensor(fin[:, 4, :], tps[0][:, 0:NBT], fin[:, 3, :], ALU.add).then_inc(sum_done, 1)

        @block.tensor
        def _(pe):
            def dense_products(base, j):
                kt, g = divmod(j, 2)
                w = width(kt)
                if j in SPLIT_WAITS:
                    pe.wait_ge(split_done, SPLIT_WAITS[j])
                if kt == D_FIRST // P and g == 0:
                    pe.wait_ge(dense_more_in, 16 * PARTS)
                if kt == (D_FIRST + D_MORE) // P and g == 0:
                    pe.wait_ge(dense_rest_in, 16 * PARTS)
                if j >= 2:
                    pe.wait_ge(x_done, base + (j - 1))
                cols = slice(kt * P, kt * P + w) if isinstance(base, int) else bass.ds(base * (P // 2) + kt * P, P)
                for q in range(HALF):
                    t = g * HALF + q
                    last = nc.tensor.matmul(rps[j % 2][:, q, 0:w], xd[0:SPLIT_K, t * P:(t + 1) * P],
                                            dense[0:SPLIT_K, cols], start=True, stop=True)
                last.then_inc(r_done, 1)

            def transposes(base, j):
                w = width(j // 2)
                pe.wait_ge(x_done, base + (j + 1))
                if j >= 2:
                    pe.wait_ge(lo_done, base + (j - 1))
                for q in range(HALF):
                    last = nc.tensor.transpose(tps[j % 2][0:w, q * P:(q + 1) * P], x[:, j % NX, q, 0:w], ident[:])
                last.then_inc(t_done, 1)

            def layer1(base, j):
                kt, g = divmod(j, 2)
                w = width(kt)
                c = kt // KPC
                if j % (2 * KPC) == 0:
                    pe.wait_ge(wlo_done, (base if isinstance(base, int) else base // (2 * KPC)) + (c + 1))
                pe.wait_ge(lo_done, base + (j + 1))
                for t in range(NHT):
                    col = kt % KPC * H1 + t * P
                    hi, lo = whi[0:w, c % NW, col:col + P], wlo[0:w, c % NW, col:col + P]
                    nc.tensor.matmul(acc[t][g][:], hi, xhi[0:w, j % NXT, :], start=(kt == 0), stop=False)
                    nc.tensor.matmul(acc[t][g][:], hi, xlo[0:w, j % NXT, :], start=False, stop=False)
                    last = nc.tensor.matmul(acc[t][g][:], lo, xhi[0:w, j % NXT, :], start=False,
                                            stop=(kt == NKT - 1))
                    if j == NU - 1:
                        last.then_inc(last_done, 1)
                if j < NU - 1:
                    last.then_inc(mm_done, 1)

            def step(base, j):
                if j + R_AHEAD < NU:
                    dense_products(base, j + R_AHEAD)
                if 0 <= j + T_AHEAD < NU:
                    transposes(base, j + T_AHEAD)
                if j >= 0:
                    layer1(base, j)

            def stay_warm(n):
                for _ in range(n):
                    nc.tensor.matmul(tps[1][:], xd[0:SPLIT_K, 0:P], xd[0:SPLIT_K, 0:HB], start=True, stop=True)

            pe.wait_ge(ident_ready, 1)
            for j in range(-R_AHEAD, TURN):
                step(0, j)
            turns = (NU - R_AHEAD) // TURN - 1
            with nc.tensor.Fori(0, turns) as turn:
                for j in range(TURN, 2 * TURN):
                    step(turn * TURN, j)
            for j in range((turns + 1) * TURN, NU):
                step(0, j)
            stay_warm(18)

            pe.wait_ge(par_in, 16)
            pe.wait_ge(par2_in, 16)
            for g in range(2):
                for t in range(NHT):
                    pe.wait_ge(h1_done[t][g], 1)
                    last = nc.tensor.matmul(rps[g][:].rearrange("p a b -> p (a b)"), w2[:, t, :],
                                            h1[:, t, g * HB:(g + 1) * HB], start=(t == 0), stop=(t == NHT - 1))
                last.then_inc(l2_done, 1)
            stay_warm(14)
            for t in range(NBT):
                nc.tensor.matmul(tps[0][:, t:t + 1], xd[0:SPLIT_K, t * P:(t + 1) * P],
                                 dense[0:SPLIT_K, FM1_COL:FM1_COL + 1], start=True, stop=False)
                pe.wait_ge(h2_done, t // HALF + 1)
                last = nc.tensor.matmul(tps[0][:, t:t + 1], h2[:, t * P:(t + 1) * P], par[:, C_WOUT:C_WOUT + 1],
                                        start=False, stop=True)
            last.then_inc(logit_done, 1)


def kernel(r_X_dense, r_X_sparse, L0_rec_fm1_emb, L0_rec_bias, L0_rec_fm1_dense_W, L0_rec_fm1_dense_b,
           L0_rec_emb_tables, L0_rec_dense_W, L0_rec_dense_b, L0_rec_W1, L0_rec_b1, L0_rec_g1, L0_rec_beta1,
           L0_rec_W2, L0_rec_b2, L0_rec_g2, L0_rec_beta2, L0_rec_Wout, L0_rec_bout):
    import numpy as np
    import concourse.bacc as bacc
    from concourse.bass_utils import run_bass_kernel_spmd

    def a(v):
        return np.asarray(v)

    def by_field(v):
        v = a(v)
        return v.reshape(F, F, D_EMB, -1).transpose(1, 0, 2, 3).reshape(K1, -1)

    table = np.concatenate([a(L0_rec_emb_tables).transpose(1, 0, 2).reshape(V, ROW), a(L0_rec_fm1_emb)], axis=1)
    w1 = np.zeros((NCH * KPC * P, H1), np.float32)
    w1[:K1] = by_field(a(L0_rec_W1).T)
    w1 = w1.reshape(NCH, KPC, P, H1).transpose(0, 2, 1, 3).reshape(NCH, P, KPC * H1)
    dw = np.zeros((DR, DW), np.float32)
    dw[:NDENSE, :K1] = by_field(L0_rec_dense_W).T
    dw[NDENSE, :K1] = by_field(L0_rec_dense_b)[:, 0]
    dw[:NDENSE, FM1_COL] = a(L0_rec_fm1_dense_W)[0]
    dw[NDENSE, FM1_COL] = a(L0_rec_fm1_dense_b)[0]
    dx = np.ones((DR, B), np.float32)
    dx[:NDENSE] = a(r_X_dense).reshape(P, NBT, NDENSE).transpose(2, 1, 0).reshape(NDENSE, B)
    x0 = np.tile(dx, (PARTS * PARTS, 1))
    d0 = np.tile(dw[:, :D_FIRST], (PARTS * PARTS, 1))
    d1 = dw[:, D_FIRST:].reshape(DR * DXP, D1C)
    xs = a(r_X_sparse).reshape(P, NBT, F).transpose(0, 2, 1).reshape(P, F * NBT)
    params = np.zeros((P, NPAR), np.float32)
    params[:, C_B1:C_B1 + NHT] = a(L0_rec_b1).reshape(NHT, P).T
    params[:, C_G1:C_G1 + NHT] = a(L0_rec_g1).reshape(NHT, P).T
    params[:, C_BETA1:C_BETA1 + NHT] = a(L0_rec_beta1).reshape(NHT, P).T
    params[:, C_B2], params[:, C_G2], params[:, C_BETA2] = a(L0_rec_b2), a(L0_rec_g2), a(L0_rec_beta2)
    params[:, C_WOUT] = a(L0_rec_Wout)[0]
    params[:, C_BIAS] = a(L0_rec_bias)[0]
    params[:, C_BOUT] = a(L0_rec_bout)[0]
    row = np.arange(SPLIT_K)
    for c, p in ((C_MASK, row // (PARTS * DR)), (C_MASK + 2, row // DR % PARTS)):
        params[:SPLIT_K, c] = np.where(p >= 1, -1.0, 0.0)
        params[:SPLIT_K, c + 1] = np.where(p >= 2, -1.0, 0.0)
    w2 = a(L0_rec_W2).T.reshape(NHT, P, H2).transpose(1, 0, 2)

    nc = bacc.Bacc("TRN2", target_bir_lowering=False, num_devices=1)
    arrays, args = {}, []
    for name, v in (("table", table), ("w1t", w1), ("x0", x0), ("d0", d0), ("d1", d1), ("xs", xs), ("params", params), ("w2t", w2)):
        arrays[name] = np.ascontiguousarray(v)
        args.append(nc.dram_tensor(name, v.shape, mybir.dt.from_np(v.dtype), kind="ExternalInput").ap())
    parts = nc.dram_tensor("parts", (PARTS, DR, DXP, D1C), mybir.dt.bfloat16, kind="Internal").ap()
    out = nc.dram_tensor("y", (P, NBT), mybir.dt.float32, kind="ExternalOutput").ap()
    recommender(nc, *args, parts, out)
    r = run_bass_kernel_spmd(nc, [arrays], core_ids=[0])
    return np.asarray(r.results[0]["y"]).reshape(B, 1)
```

```python
import concourse.bass as bass
from concourse import mybir
from contextlib import ExitStack

P = 128
B = 1024
NBT = B // P
HALF = NBT // 2
NPAIR = NBT // 2
HB = B // 2
F = 26
V = F * 1000
D_EMB = 16
ROW = F * D_EMB
TROW = ROW + 1
K1 = F * ROW
H1, H2 = 256, 128
NHT = H1 // P
NDENSE = 13
DR = NDENSE + 1
EPS = 1e-5
NKT = -(-K1 // P)
NU = 2 * NKT
PARTS = 3
SPLIT_K = PARTS * PARTS * DR
FM1_COL = K1
DW = K1 + 8
DXP = 8
D_FIRST = 8 * P
D1C = (DW - D_FIRST) // DXP
D_PIECE = D_FIRST
SQ = F // 2
SPLITS = (("d", 0, 2 * P), ("x", 0, HB), ("x", HB, B), ("d", 2 * P, D_FIRST))
REST_REM = (0, 3)
REST_PART = (1, 3)
NA, NX, NXT, NWRAW, NW = 3, 4, 4, 4, 4
KPC = 2
NCH = -(-NKT // KPC)
R_AHEAD, T_AHEAD = 4, 2
W_AHEAD = 8
TURN = 2 * KPC * NW
SPLIT_WAITS = {0: 2, 2: 3, 4: 4}
EARLY = 2
WARM_START = {0: 1, 1: 1}
H1_ACT, H1_DVE = ((0, 0), (0, 1), (1, 1)), ((1, 0),)
C_B1, C_G1, C_BETA1, C_B2, C_G2, C_BETA2, C_WOUT, C_BIAS, C_BOUT = 0, 2, 4, 6, 7, 8, 9, 10, 11
C_MASK, NPAR = 12, 16


def segments(kt):
    k, end, out = kt * P, min((kt + 1) * P, K1), []
    while k < end:
        f, c = divmod(k, ROW)
        n = min(end - k, ROW - c)
        out.append((f, c, k - kt * P, n))
        k += n
    return out


def width(kt):
    return min(P, K1 - kt * P)


def unit(j):
    return (j % 2, j // 2) if j < 4 else divmod(j, 2)


def first_unit(f):
    return 2 * (f * ROW // P)


def last_unit(f):
    return 2 * (((f + 1) * ROW - 1) // P) + 1


def fm2_pairs(v):
    out = []
    for f in range(1, F):
        a = first_unit(f)
        b = first_unit(f + 1) if f + 1 < F else NU
        if a <= v < b:
            n = b - a
            out += [(f, t) for t in range(-(-NPAIR * (v - a) // n), -(-NPAIR * (v - a + 1) // n))]
    return out


def pair_count(f, t):
    return (f - 1) * NPAIR + t + 1


def keeps_at(v):
    out = []
    if v == 3:
        out += [(0, 0), (0, 1)]
    for f, t in fm2_pairs(v - 1):
        if (t + 1) * 2 % HALF == 0:
            out.append((f, (t + 1) * 2 // HALF - 1))
    return out


def recommender(nc, table, w1t, x0, d0, d1, xs, params, w2t, parts, out):
    f32, f32r, bf16, i32 = mybir.dt.float32, mybir.dt.float32r, mybir.dt.bfloat16, mybir.dt.int32
    ALU = mybir.AluOpType
    ACT = mybir.ActivationFunctionType
    AX = mybir.AxisListType

    ctx = ExitStack()
    with ctx:
        def sb(name, shape, dt):
            return ctx.enter_context(nc.sbuf_tensor(name, shape, dt))

        def pb(name, shape, dt):
            return ctx.enter_context(nc.psum_tensor(name, shape, dt))

        def sem(name):
            return ctx.enter_context(nc.semaphore(name))

        gath = sb("gath", [P, NA, NBT, TROW], f32)
        kept = sb("kept", [P, NBT, SQ, SQ, D_EMB], f32)
        x = sb("x", [P, NX, HALF, P], f32)
        xhi = sb("xhi", [P, NXT, HB], f32r)
        xlo = sb("xlo", [P, NXT, HB], f32r)
        wraw = sb("wraw", [P, NWRAW, KPC * H1], f32)
        whi = sb("whi", [P, NW, KPC * H1], f32r)
        wlo = sb("wlo", [P, NW, KPC * H1], f32r)
        dense = sb("dense", [P, DW], bf16)
        xd = sb("xd", [P, B], bf16)
        prod = sb("prod", [P, 2, 2, (F - 1) * D_EMB], f32)
        fm2 = sb("fm2", [P, NBT, F - 1], f32)
        fm1 = sb("fm1", [P, F, NBT], f32)
        idx = sb("idx", [P, F, NBT], i32)
        par = sb("par", [P, NPAR], f32)
        w2 = sb("w2", [P, NHT, H2], f32)
        ident = sb("ident", [P, P], f32)
        stats = sb("stats", [P, NHT + 1, 2, 6], f32)
        mv = sb("mv", [P, NHT + 1, 2], f32)
        bn = sb("bn", [P, 9, NHT + 1], f32)
        fin = sb("fin", [P, 6, NBT], f32)
        warm = sb("warm", [P, 3], f32)

        kept_flat = kept[:].rearrange("p a b c d -> p (a b c d)")
        def room(at, n):
            return kept_flat[:, at:at + n]

        raw = {"x": room(0, B), "d": room(1024, D_FIRST)}
        rem = {"x": room(2048, B), "d": room(3072, D_FIRST)}
        head = {"x": room(4096, B // 2).bitcast(bf16), "d": room(4608, D_FIRST // 2).bitcast(bf16)}
        mid = {"x": room(5120, B // 2).bitcast(bf16), "d": room(5632, D_FIRST // 2).bitcast(bf16)}
        part = dense[:, D_FIRST:D_FIRST + PARTS * D1C].rearrange("p (j c) -> p j c", j=PARTS)
        left_at = D_FIRST + (PARTS + 1) * D1C // 2 * 2
        left = dense[:, left_at:left_at + 2 * D1C].bitcast(f32)
        xi = room(14336, F * NBT).bitcast(i32)
        of = room(14592, F * NBT).bitcast(i32)
        xf = room(14848, F * NBT)
        neg = room(15104, F * NBT)
        h1 = room(0, NHT * B).rearrange("p (t b) -> p t b", t=NHT)
        h2 = room(2048, B)

        acc = [[pb(f"acc{t}{g}", [P, HB], f32) for g in range(2)] for t in range(NHT)]
        rps = [pb(f"rps{i}", [P, HALF, P], f32) for i in range(2)]
        tps = [pb(f"tps{i}", [P, HB], f32) for i in range(2)]

        x0_in, d0_in, d1_in, xs_in, par_in, par2_in = (
            sem(n) for n in ("x0_in", "d0_in", "d1_in", "xs_in", "par_in", "par2_in"))
        idx_ready, offs_ready, part_ready, rest_ready, parts_out = (
            sem(n) for n in ("idx_ready", "offs_ready", "part_ready", "rest_ready", "parts_out"))
        head_done, rem_done, mid_done, split_done = (
            sem(n) for n in ("head_done", "rem_done", "mid_done", "split_done"))
        dense_in = sem("dense_in")
        w_in = [sem(f"w_in{i}") for i in range(NWRAW)]
        gathered = [[sem(f"gathered{i}_{g}") for g in range(2)] for i in range(NA)]
        ident0, ident_ready = sem("ident0"), sem("ident_ready")
        r_done, x_done, t_done, hi_done, lo_done, mm_done = (
            sem(n) for n in ("r_done", "x_done", "t_done", "hi_done", "lo_done", "mm_done"))
        whi_done, wlo_done = sem("whi_done"), sem("wlo_done")
        prod_done, acc_done, keep_done, fm1_done = sem("prod_done"), sem("acc_done"), sem("keep_done"), sem("fm1_done")
        last_done = sem("last_done")
        step_done, warm_ready, std_done, l2_done, h2_done, logit_done = (
            sem(n) for n in ("step_done", "warm_ready", "std_done", "l2_done", "h2_done", "logit_done"))
        h1_done = [[sem(f"h1_done{t}{g}") for g in range(2)] for t in range(NHT)]
        var_done, norm_done, sum_done, y_done, y_out = (
            sem(n) for n in ("var_done", "norm_done", "sum_done", "y_done", "y_out"))
        block = ctx.enter_context(nc.Block())

        def keep_count(f):
            return 2 * (f + 1)

        @block.sync
        def _(sp):
            sp.dma_start(xi, xs).then_inc(xs_in, 16)
            sp.dma_start(raw["x"][0:SPLIT_K, :], x0).then_inc(x0_in, 16)
            for c in range(NWRAW):
                if 1 <= c <= 2:
                    sp.wait_ge(gathered[0][c - 1], 16 * HALF)
                sp.dma_start(wraw[:, c, :], w1t[c]).then_inc(w_in[c], 16)
            sp.dma_start(w2[:], w2t).then_inc(par2_in, 16)

            def load_w(c):
                sp.wait_ge(wlo_done, c - NWRAW + 1)
                sp.dma_start(wraw[:, c % NWRAW, :], w1t[c]).then_inc(w_in[c % NWRAW], 16)

            load_w(NWRAW)
            sp.wait_ge(part_ready, PARTS)
            sp.dma_start(parts.rearrange("j r g c -> (r g) j c"), part[0:DR * DXP, :, :]).then_inc(parts_out, 16)
            sp.wait_ge(parts_out, 16)
            rows = parts.rearrange("j r g c -> (j r) (g c)")

            def load_dense(at, n):
                for i in range(PARTS):
                    to = slice(i * PARTS * DR, (i + 1) * PARTS * DR)
                    if isinstance(at, int):
                        dst, src = dense[to, at:at + n], rows[:, at - D_FIRST:at - D_FIRST + n]
                    else:
                        dst, src = dense[to, bass.ds(at, n)], rows[:, bass.ds(at - D_FIRST, n)]
                    sp.dma_start(dst, src).then_inc(dense_in, 16)

            load_dense(D_FIRST, D_PIECE)
            first = NWRAW + 3
            for c in range(NWRAW + 1, first):
                load_w(c)
            turns = (NCH - first) // NWRAW - 1
            with nc.sync.Fori(0, turns) as turn:
                base = turn * NWRAW
                for j in range(first, first + NWRAW):
                    sp.wait_ge(wlo_done, base + (j - NWRAW + 1))
                    sp.dma_start(wraw[:, j % NWRAW, :], w1t[bass.ds(base + j, 1)].rearrange("c p h -> p (c h)")).then_inc(
                        w_in[j % NWRAW], 16)
                sp.wait_ge(dense_in, turn * (16 * PARTS) + 16 * PARTS)
                load_dense(turn * D_PIECE + (D_FIRST + D_PIECE), D_PIECE)
            for c in range(first + turns * NWRAW, NCH):
                load_w(c)
            sp.wait_ge(dense_in, (turns + 1) * 16 * PARTS)
            at = D_FIRST + (turns + 1) * D_PIECE
            load_dense(at, DW - at)
            sp.wait_ge(y_done, 1)
            sp.dma_start(out, fin[:, 5, :]).then_inc(y_out, 16)
            sp.wait_ge(y_out, 16)

        @block.gpsimd
        def _(pool):
            nc.gpsimd.iota(of, pattern=[[V // F, F], [0, NBT]], base=0, channel_multiplier=0).then_inc(offs_ready, 1)
            nc.gpsimd.memset(ident[:], 0.0).then_inc(ident0, 1)
            pool.wait_ge(ident0, 1)
            nc.gpsimd.affine_select(out=ident[:], in_=ident[:], compare_op=ALU.not_equal, fill=1.0, base=0,
                                    pattern=[[-1, P]], channel_multiplier=1).then_inc(ident_ready, 1)
            chunk = 0
            pool.wait_ge(idx_ready, 1)
            for f in range(F + NA):
                if f == 1:
                    pool.wait_ge(idx_ready, 2)
                while chunk < NCH and (f >= F or KPC * 2 * chunk <= f * 2 * ROW // P - 5):
                    if chunk >= NW:
                        pool.wait_ge(mm_done, 2 * KPC * (chunk - NW + 1))
                    pool.wait_ge(whi_done, chunk + 1)
                    nc.gpsimd.tensor_tensor(wlo[:, chunk % NW, :], wraw[:, chunk % NWRAW, :],
                                            whi[:, chunk % NW, :].bitcast(f32), ALU.subtract).then_inc(wlo_done, 1)
                    chunk += 1
                if f >= NA:
                    old = f - NA
                    pool.wait_ge(x_done, last_unit(old) + 1)
                    pool.wait_ge(keep_done, keep_count(old))
                    nc.gpsimd.tensor_copy(fm1[:, old, :], gath[:, old % NA, :, ROW]).then_inc(fm1_done, 1)
                if f < F:
                    if f >= NA:
                        pool.wait_ge(fm1_done, f - NA + 1)
                    for t in range(NBT):
                        nc.gpsimd.indirect_dma_start(
                            gath[:, f % NA, t, :], None, table,
                            bass.IndirectOffsetOnAxis(ap=idx[:, f, t:t + 1], axis=0)).then_inc(gathered[f % NA][t // HALF], 16)

        @block.scalar
        def _(act):
            def make_whi(c):
                act.wait_ge(w_in[c % NWRAW], 16 * (c // NWRAW + 1))
                if c >= NW:
                    act.wait_ge(mm_done, 2 * KPC * (c - NW + 1))
                nc.scalar.copy(whi[:, c % NW, :], wraw[:, c % NWRAW, :]).then_inc(whi_done, 1)

            def accumulate(f, t):
                act.wait_ge(prod_done, pair_count(f, t))
                for i in range(2):
                    row = prod[:, pair_count(f, t) % 2, i, 0:f * D_EMB]
                    last = nc.scalar.activation(row, row, ACT.Copy, accum_out=fm2[:, 2 * t + i, f - 1:f])
                last.then_inc(acc_done, 1)

            def keep(f, g):
                tiles = slice(g * HALF, (g + 1) * HALF)
                src = gath[:, f % NA, tiles, 0:ROW].rearrange("p b (t d) -> p b t d", d=D_EMB)
                if f >= 1:
                    act.wait_ge(prod_done, pair_count(f, (g + 1) * HALF // 2 - 1))
                if f == 0:
                    act.wait_ge(gathered[0][g], 16 * HALF)
                    act.wait_ge(split_done, len(SPLITS))
                    act.wait_ge(idx_ready, 2)
                if f < SQ:
                    last = nc.scalar.copy(kept[:, tiles, f, :, :], src[:, :, SQ:F, :])
                    if f + 1 < SQ:
                        last = nc.scalar.copy(kept[:, tiles, f + 1:SQ, f, :], src[:, :, f + 1:SQ, :])
                elif f + 1 < F:
                    c = f - SQ
                    last = nc.scalar.copy(kept[:, tiles, c + 1:SQ, c, :], src[:, :, f + 1:F, :])
                else:
                    last = act.nop()
                last.then_inc(keep_done, 1)

            act.dma_start(par[:], params).then_inc(par_in, 16)
            act.dma_start(raw["d"][0:SPLIT_K, :], d0).then_inc(d0_in, 16)
            act.wait_ge(warm_ready, 1)
            nc.scalar.activation(warm[:, 1:2], warm[:, 0:1], ACT.Sqrt)

            def split_head(n):
                of_, a, b = SPLITS[n]
                act.wait_ge(x0_in if of_ == "x" else d0_in, 16)
                nc.scalar.copy(head[of_][0:SPLIT_K, a:b], raw[of_][0:SPLIT_K, a:b]).then_inc(head_done, 1)

            def split_mid(n):
                of_, a, b = SPLITS[n]
                act.wait_ge(rem_done, n + 1)
                nc.scalar.copy(mid[of_][0:SPLIT_K, a:b], rem[of_][0:SPLIT_K, a:b]).then_inc(mid_done, 1)

            def rest_part(j):
                if j == 0:
                    act.wait_ge(d1_in, 16)
                else:
                    act.wait_ge(rest_ready, j)
                nc.scalar.copy(part[0:DR * DXP, j, :], left[0:DR * DXP, :]).then_inc(part_ready, 1)

            split_head(0)
            split_head(1)
            split_mid(0)
            act.dma_start(left[0:DR * DXP, :], d1).then_inc(d1_in, 16)
            split_head(2)
            split_mid(1)
            split_mid(2)
            split_head(3)
            make_whi(0)
            rest_part(0)
            chunk = 1
            for s in range(-R_AHEAD, NU):
                u = s + T_AHEAD
                if 0 <= u < NU:
                    w = width(unit(u)[0])
                    act.wait_ge(t_done, u + 1)
                    if u >= NXT:
                        act.wait_ge(mm_done, u - NXT + 1)
                    nc.scalar.copy(xhi[0:w, u % NXT, :], tps[u % 2][0:w, :]).then_inc(hi_done, 1)
                if u == 0:
                    split_mid(3)
                while chunk < NCH and max(1 - T_AHEAD, 2 * KPC * chunk - W_AHEAD) <= s:
                    make_whi(chunk)
                    chunk += 1
                if s in REST_PART:
                    rest_part(1 + REST_PART.index(s))
                for f, g in keeps_at(s + R_AHEAD):
                    keep(f, g)
                for f, t in fm2_pairs(s + R_AHEAD - 1):
                    accumulate(f, t)

            act.wait_ge(var_done, 1)
            nc.scalar.activation(bn[:, 1, 0:NHT], bn[:, 0, 0:NHT], ACT.Sqrt).then_inc(std_done, 1)
            act.wait_ge(norm_done, 1)
            act.wait_ge(prod_done, pair_count(F - 1, NPAIR - 1))
            for t, g in H1_ACT:
                nc.scalar.activation(h1[:, t, g * HB:(g + 1) * HB], acc[t][g][:], ACT.Relu, bias=bn[:, 6, t:t + 1],
                                     scale=bn[:, 5, t:t + 1]).then_inc(h1_done[t][g], 1)
            act.wait_ge(var_done, 2)
            nc.scalar.activation(bn[:, 1, NHT:NHT + 1], bn[:, 0, NHT:NHT + 1], ACT.Sqrt).then_inc(std_done, 1)
            nc.scalar.activation(warm[:, 2:3], warm[:, 0:1], ACT.Sigmoid)
            act.wait_ge(norm_done, 2)
            for g in range(2):
                nc.scalar.activation(h2[:, g * HB:(g + 1) * HB], rps[g][:].rearrange("p a b -> p (a b)"), ACT.Relu,
                                     bias=bn[:, 6, NHT:NHT + 1], scale=bn[:, 5, NHT:NHT + 1]).then_inc(h2_done, 1)
            act.wait_ge(sum_done, 1)
            nc.scalar.activation(fin[:, 5, :], fin[:, 4, :], ACT.Sigmoid).then_inc(y_done, 1)

        @block.vector
        def _(dve):
            steps = [0]

            def link(ins):
                steps[0] += 1
                ins.then_inc(step_done, 1)
                dve.wait_ge(step_done, steps[0])

            nc.vector.memset(warm[:, 0:1], 1.0).then_inc(warm_ready, 1)
            def split_rem(n):
                of_, a, b = SPLITS[n]
                m = C_MASK + (0 if of_ == "x" else 2)
                dve.wait_ge(head_done, n + 1)
                nc.vector.scalar_tensor_tensor(
                    out=rem[of_][0:SPLIT_K, a:b], in0=head[of_][0:SPLIT_K, a:b], scalar=par[0:SPLIT_K, m:m + 1],
                    in1=raw[of_][0:SPLIT_K, a:b], op0=ALU.mult, op1=ALU.add).then_inc(rem_done, 1)

            def split_last(n):
                of_, a, b = SPLITS[n]
                m = C_MASK + (1 if of_ == "x" else 3)
                dve.wait_ge(mid_done, n + 1)
                nc.vector.scalar_tensor_tensor(
                    out={"x": xd, "d": dense}[of_][0:SPLIT_K, a:b], in0=mid[of_][0:SPLIT_K, a:b],
                    scalar=par[0:SPLIT_K, m:m + 1], in1=rem[of_][0:SPLIT_K, a:b], op0=ALU.mult,
                    op1=ALU.add).then_inc(split_done, 1)

            def rest_rem(j):
                dve.wait_ge(part_ready, j + 1)
                rows = left[0:DR * DXP, :]
                nc.vector.tensor_tensor(rows, rows, part[0:DR * DXP, j, :], ALU.subtract).then_inc(rest_ready, 1)

            dve.wait_ge(xs_in, 16)
            dve.wait_ge(offs_ready, 1)
            for a, b in ((0, NBT), (NBT, F * NBT)):
                link(nc.vector.tensor_tensor(xf[:, a:b], xi[:, a:b], of[:, a:b], ALU.add))
                link(nc.vector.tensor_scalar(neg[:, a:b], xf[:, a:b], 0.0, float(V), ALU.is_lt, ALU.mult))
                link(nc.vector.tensor_tensor(xf[:, a:b], xf[:, a:b], neg[:, a:b], ALU.add))
                nc.vector.tensor_scalar(idx[:].rearrange("p f t -> p (f t)")[:, a:b], xf[:, a:b], 0.0, float(V - 1),
                                        ALU.max, ALU.min).then_inc(idx_ready, 1)
            dve.wait_ge(par_in, 16)
            split_rem(0)
            split_rem(1)
            split_last(0)
            split_rem(2)
            split_last(1)
            split_last(2)

            def multiply(f, t):
                tiles = slice(2 * t, 2 * t + 2)
                a = gath[:, f % NA, tiles, 0:ROW].rearrange("p b (t d) -> p b t d", d=D_EMB)
                dve.wait_ge(keep_done, keep_count(f - 1) - 1 + 2 * t // HALF)
                n = pair_count(f, t)
                if n > 2:
                    dve.wait_ge(acc_done, n - 2)
                o = prod[:, n % 2, :, 0:f * D_EMB].rearrange("p b (t d) -> p b t d", d=D_EMB)
                if f < SQ:
                    last = nc.vector.tensor_tensor(o, a[:, :, 0:f, :], kept[:, tiles, f, 0:f, :], ALU.mult)
                else:
                    c = f - SQ
                    last = nc.vector.tensor_tensor(o[:, :, 0:SQ, :], a[:, :, 0:SQ, :], kept[:, tiles, 0:SQ, c, :],
                                                   ALU.mult)
                    if c:
                        last = nc.vector.tensor_tensor(o[:, :, SQ:f, :], a[:, :, SQ:f, :],
                                                       kept[:, tiles, c, 0:c, :], ALU.mult)
                last.then_inc(prod_done, 1)

            def make_x(u):
                kt, g = unit(u)
                dve.wait_ge(r_done, u + 1)
                if u >= NX:
                    dve.wait_ge(t_done, u - NX + 1)
                for f, c, o, n in segments(kt):
                    dve.wait_ge(gathered[f % NA][g], 16 * HALF * (f // NA + 1))
                    last = nc.vector.scalar_tensor_tensor(
                        out=x[:, u % NX, :, o:o + n], in0=rps[u % 2][:, :, o:o + n], scalar=0.0,
                        in1=gath[:, f % NA, g * HALF:(g + 1) * HALF, c:c + n], op0=ALU.max, op1=ALU.add)
                last.then_inc(x_done, 1)

            def make_lo(u):
                w = width(unit(u)[0])
                dve.wait_ge(hi_done, u + 1)
                nc.vector.tensor_tensor(xlo[0:w, u % NXT, :], tps[u % 2][0:w, :],
                                        xhi[0:w, u % NXT, :].bitcast(f32), ALU.subtract).then_inc(lo_done, 1)

            make_x(0)
            make_x(1)
            split_rem(3)
            make_lo(0)
            split_last(3)
            make_lo(1)
            for s in range(EARLY - R_AHEAD, NU):
                if s in REST_REM:
                    rest_rem(REST_REM.index(s))
                u = s + R_AHEAD
                if u < NU:
                    make_x(u)
                    for f, t in fm2_pairs(u):
                        multiply(f, t)
                if EARLY <= s + T_AHEAD < NU:
                    make_lo(s + T_AHEAD)

            def normalise(first, n, bias, g, beta):
                c = slice(first, first + n)
                raw_mean, var = mv[:, c, 0], mv[:, c, 1]
                nc.vector.tensor_scalar_add(bn[:, 0, c], var, EPS).then_inc(var_done, 1)
                link(nc.vector.tensor_tensor(bn[:, 8, c], raw_mean, par[:, bias:bias + n], ALU.add))
                nc.vector.tensor_tensor(bn[:, 7, c], par[:, bias:bias + n], bn[:, 8, c], ALU.subtract)
                nc.vector.tensor_scalar_mul(bn[:, 4, c], bn[:, 0, c], -0.5)
                dve.wait_ge(std_done, 1 if first == 0 else 2)
                link(nc.vector.reciprocal(bn[:, 2, c], bn[:, 1, c]))
                nc.vector.tensor_tensor(bn[:, 1, c], bn[:, 2, c], par[:, g:g + n], ALU.mult)
                for t in range(first, first + n):
                    last = nc.vector.scalar_tensor_tensor(out=bn[:, 3, t:t + 1], in0=bn[:, 4, t:t + 1],
                                                          scalar=bn[:, 2, t:t + 1], in1=bn[:, 2, t:t + 1],
                                                          op0=ALU.mult, op1=ALU.mult)
                link(last)
                link(nc.vector.scalar_tensor_tensor(out=bn[:, 5, c], in0=bn[:, 3, c], scalar=1.5, in1=bn[:, 1, c],
                                                    op0=ALU.add, op1=ALU.mult))
                for t in range(first, first + n):
                    last = nc.vector.scalar_tensor_tensor(
                        out=bn[:, 6, t:t + 1], in0=bn[:, 7, t:t + 1], scalar=bn[:, 5, t:t + 1],
                        in1=par[:, beta + t - first:beta + t - first + 1], op0=ALU.mult, op1=ALU.add)
                link(last)
                dve.sem_inc(norm_done, 1)

            for g in range(2):
                for t in range(NHT):
                    if g == 0:
                        dve.wait_ge(mm_done, NU - 1)
                    else:
                        dve.wait_ge(last_done, t + 1)
                    last = nc.vector.bn_stats(stats[:, t, g, :], acc[t][g][:])
            link(last)
            for t in range(NHT):
                last = nc.vector.bn_aggr(mv[:, t, :], stats[:, t, :, :])
            link(last)
            normalise(0, NHT, C_B1, C_G1, C_BETA1)
            for t, g in H1_DVE:
                o = h1[:, t, g * HB:(g + 1) * HB]
                link(nc.vector.tensor_scalar(o, acc[t][g][:], bn[:, 5, t:t + 1], bn[:, 6, t:t + 1], ALU.mult, ALU.add))
                nc.vector.tensor_scalar_max(o, o, 0.0).then_inc(h1_done[t][g], 1)
            dve.wait_ge(fm1_done, F)
            dve.wait_ge(acc_done, pair_count(F - 1, NPAIR - 1))
            nc.vector.tensor_reduce(fin[:, 0, :], fm1[:].rearrange("p f t -> p t f"), AX.X, ALU.add)
            link(nc.vector.tensor_reduce(fin[:, 1, :], fm2[:], AX.X, ALU.add))
            link(nc.vector.tensor_tensor(fin[:, 2, :], fin[:, 0, :], fin[:, 1, :], ALU.add))
            link(nc.vector.tensor_scalar(fin[:, 3, :], fin[:, 2, :], par[:, C_BIAS:C_BIAS + 1],
                                         par[:, C_BOUT:C_BOUT + 1], ALU.add, ALU.add))
            for g in range(2):
                dve.wait_ge(l2_done, g + 1)
                last = nc.vector.bn_stats(stats[:, NHT, g, :], rps[g][:].rearrange("p a b -> p (a b)"))
            link(last)
            link(nc.vector.bn_aggr(mv[:, NHT, :], stats[:, NHT, :, :]))
            normalise(NHT, 1, C_B2, C_G2, C_BETA2)
            dve.wait_ge(logit_done, 1)
            nc.vector.tensor_tensor(fin[:, 4, :], tps[0][:, 0:NBT], fin[:, 3, :], ALU.add).then_inc(sum_done, 1)

        @block.tensor
        def _(pe):
            def stay_warm(n):
                for _ in range(n):
                    nc.tensor.matmul(tps[1][:], xd[0:SPLIT_K, 0:P], xd[0:SPLIT_K, 0:HB], start=True, stop=True)

            def dense_products(base, j):
                kt, g = unit(j)
                w = width(kt)
                if j in SPLIT_WAITS:
                    pe.wait_ge(split_done, SPLIT_WAITS[j])
                if kt >= D_FIRST // P and j % (2 * D_PIECE // P) == 0:
                    pe.wait_ge(dense_in, base * (16 * PARTS // TURN) + 16 * PARTS * (kt // (D_PIECE // P)))
                if j >= 2:
                    pe.wait_ge(x_done, base + (j - 1))
                cols = slice(kt * P, kt * P + w) if isinstance(base, int) else bass.ds(base * (P // 2) + kt * P, P)
                for q in range(HALF):
                    t = g * HALF + q
                    last = nc.tensor.matmul(rps[j % 2][:, q, 0:w], xd[0:SPLIT_K, t * P:(t + 1) * P],
                                            dense[0:SPLIT_K, cols], start=True, stop=True)
                last.then_inc(r_done, 1)

            def transposes(base, j):
                w = width(unit(j)[0])
                pe.wait_ge(x_done, base + (j + 1))
                if j >= 2:
                    pe.wait_ge(lo_done, base + (j - 1))
                for q in range(HALF):
                    last = nc.tensor.transpose(tps[j % 2][0:w, q * P:(q + 1) * P], x[:, j % NX, q, 0:w], ident[:])
                last.then_inc(t_done, 1)

            def layer1(base, j):
                kt, g = unit(j)
                w = width(kt)
                c = kt // KPC
                if j % (2 * KPC) == 0:
                    pe.wait_ge(wlo_done, (base if isinstance(base, int) else base // (2 * KPC)) + (c + 1))
                pe.wait_ge(lo_done, base + (j + 1))
                for t in range(NHT):
                    col = kt % KPC * H1 + t * P
                    hi, lo = whi[0:w, c % NW, col:col + P], wlo[0:w, c % NW, col:col + P]
                    nc.tensor.matmul(acc[t][g][:], hi, xhi[0:w, j % NXT, :], start=(kt == 0), stop=False)
                    nc.tensor.matmul(acc[t][g][:], hi, xlo[0:w, j % NXT, :], start=False, stop=False)
                    last = nc.tensor.matmul(acc[t][g][:], lo, xhi[0:w, j % NXT, :], start=False,
                                            stop=(kt == NKT - 1))
                    if j == NU - 1:
                        last.then_inc(last_done, 1)
                if j < NU - 1:
                    last.then_inc(mm_done, 1)

            def step(base, j):
                if j + R_AHEAD < NU:
                    dense_products(base, j + R_AHEAD)
                if 0 <= j + T_AHEAD < NU:
                    transposes(base, j + T_AHEAD)
                if j >= EARLY:
                    layer1(base, j)

            pe.wait_ge(ident_ready, 1)
            for j in range(-R_AHEAD, TURN):
                if j == 0:
                    for i in range(EARLY):
                        layer1(0, i)
                step(0, j)
                if j + R_AHEAD in WARM_START:
                    stay_warm(WARM_START[j + R_AHEAD])
            turns = (NU - R_AHEAD) // TURN - 1
            with nc.tensor.Fori(0, turns) as turn:
                for j in range(TURN, 2 * TURN):
                    step(turn * TURN, j)
            for j in range((turns + 1) * TURN, NU):
                step(0, j)
            stay_warm(18)

            pe.wait_ge(par_in, 16)
            pe.wait_ge(par2_in, 16)
            for g in range(2):
                for t in range(NHT):
                    pe.wait_ge(h1_done[t][g], 1)
                    last = nc.tensor.matmul(rps[g][:].rearrange("p a b -> p (a b)"), w2[:, t, :],
                                            h1[:, t, g * HB:(g + 1) * HB], start=(t == 0), stop=(t == NHT - 1))
                last.then_inc(l2_done, 1)
            stay_warm(14)
            for t in range(NBT):
                nc.tensor.matmul(tps[0][:, t:t + 1], xd[0:SPLIT_K, t * P:(t + 1) * P],
                                 dense[0:SPLIT_K, FM1_COL:FM1_COL + 1], start=True, stop=False)
                pe.wait_ge(h2_done, t // HALF + 1)
                last = nc.tensor.matmul(tps[0][:, t:t + 1], h2[:, t * P:(t + 1) * P], par[:, C_WOUT:C_WOUT + 1],
                                        start=False, stop=True)
            last.then_inc(logit_done, 1)


def kernel(r_X_dense, r_X_sparse, L0_rec_fm1_emb, L0_rec_bias, L0_rec_fm1_dense_W, L0_rec_fm1_dense_b,
           L0_rec_emb_tables, L0_rec_dense_W, L0_rec_dense_b, L0_rec_W1, L0_rec_b1, L0_rec_g1, L0_rec_beta1,
           L0_rec_W2, L0_rec_b2, L0_rec_g2, L0_rec_beta2, L0_rec_Wout, L0_rec_bout):
    import numpy as np
    import concourse.bacc as bacc
    from concourse.bass_utils import run_bass_kernel_spmd

    def a(v):
        return np.asarray(v)

    def by_field(v):
        v = a(v)
        return v.reshape(F, F, D_EMB, -1).transpose(1, 0, 2, 3).reshape(K1, -1)

    table = np.concatenate([a(L0_rec_emb_tables).transpose(1, 0, 2).reshape(V, ROW), a(L0_rec_fm1_emb)], axis=1)
    w1 = np.zeros((NCH * KPC * P, H1), np.float32)
    w1[:K1] = by_field(a(L0_rec_W1).T)
    w1 = w1.reshape(NCH, KPC, P, H1).transpose(0, 2, 1, 3).reshape(NCH, P, KPC * H1)
    dw = np.zeros((DR, DW), np.float32)
    dw[:NDENSE, :K1] = by_field(L0_rec_dense_W).T
    dw[NDENSE, :K1] = by_field(L0_rec_dense_b)[:, 0]
    dw[:NDENSE, FM1_COL] = a(L0_rec_fm1_dense_W)[0]
    dw[NDENSE, FM1_COL] = a(L0_rec_fm1_dense_b)[0]
    dx = np.ones((DR, B), np.float32)
    dx[:NDENSE] = a(r_X_dense).reshape(P, NBT, NDENSE).transpose(2, 1, 0).reshape(NDENSE, B)
    x0 = np.tile(dx, (PARTS * PARTS, 1))
    d0 = np.tile(dw[:, :D_FIRST], (PARTS * PARTS, 1))
    d1 = dw[:, D_FIRST:].reshape(DR * DXP, D1C)
    xs = a(r_X_sparse).reshape(P, NBT, F).transpose(0, 2, 1).reshape(P, F * NBT)
    params = np.zeros((P, NPAR), np.float32)
    params[:, C_B1:C_B1 + NHT] = a(L0_rec_b1).reshape(NHT, P).T
    params[:, C_G1:C_G1 + NHT] = a(L0_rec_g1).reshape(NHT, P).T
    params[:, C_BETA1:C_BETA1 + NHT] = a(L0_rec_beta1).reshape(NHT, P).T
    params[:, C_B2], params[:, C_G2], params[:, C_BETA2] = a(L0_rec_b2), a(L0_rec_g2), a(L0_rec_beta2)
    params[:, C_WOUT] = a(L0_rec_Wout)[0]
    params[:, C_BIAS] = a(L0_rec_bias)[0]
    params[:, C_BOUT] = a(L0_rec_bout)[0]
    row = np.arange(SPLIT_K)
    for c, p in ((C_MASK, row // (PARTS * DR)), (C_MASK + 2, row // DR % PARTS)):
        params[:SPLIT_K, c] = np.where(p >= 1, -1.0, 0.0)
        params[:SPLIT_K, c + 1] = np.where(p >= 2, -1.0, 0.0)
    w2 = a(L0_rec_W2).T.reshape(NHT, P, H2).transpose(1, 0, 2)

    nc = bacc.Bacc("TRN2", target_bir_lowering=False, num_devices=1)
    arrays, args = {}, []
    for name, v in (("table", table), ("w1t", w1), ("x0", x0), ("d0", d0), ("d1", d1), ("xs", xs), ("params", params), ("w2t", w2)):
        arrays[name] = np.ascontiguousarray(v)
        args.append(nc.dram_tensor(name, v.shape, mybir.dt.from_np(v.dtype), kind="ExternalInput").ap())
    parts = nc.dram_tensor("parts", (PARTS, DR, DXP, D1C), mybir.dt.bfloat16, kind="Internal").ap()
    out = nc.dram_tensor("y", (P, NBT), mybir.dt.float32, kind="ExternalOutput").ap()
    recommender(nc, *args, parts, out)
    r = run_bass_kernel_spmd(nc, [arrays], core_ids=[0])
    return np.asarray(r.results[0]["y"]).reshape(B, 1)
```
